# Optimizing a Trainium2 kernel written in Bass

```python
import numpy as np
import jax
import jax.numpy as jnp

def _softmax(x, axis=-1):
    return jax.nn.softmax(x, axis=axis)

def _gelu(x):
    return jax.nn.gelu(x, approximate=True)

def _silu(x):
    return jax.nn.silu(x)

def _sigmoid(x):
    return jax.nn.sigmoid(x)

def _layernorm(x, axis=-1, eps=1e-05):
    m = jnp.mean(x, axis=axis, keepdims=True)
    v = jnp.var(x, axis=axis, keepdims=True)
    return (x - m) / jnp.sqrt(v + eps)

def _scatter_add(tgt, idx, src, axis=0):
    return tgt.at[idx].add(src)

def _segment_sum(src, seg, n):
    return jax.ops.segment_sum(src, seg, n)
kernel_name = 'mk_adj_resnorm_d1_adj_r2_22cf1c'

def setup_inputs(seed: int=0):
    np.random.seed(seed)
    _w = jnp.asarray

    def _rec_inputs():
        import jax
        import jax.numpy as jnp
        _gk = jax.random.key(seed)
        x = -0.0005207 + 1.001 * jax.random.normal(jax.random.fold_in(_gk, 1), (8192, 128), jnp.float32)
        _w = (1.0 + jnp.arange(8192, dtype=jnp.float32)) ** (-0.5)
        _w = _w / _w.mean()
        _pij = jnp.clip(0.00195312 * _w[:, None] * _w[None, :], 0.0, 1.0)
        _a = jax.random.uniform(jax.random.fold_in(_gk, 2), (8192, 8192)) < _pij
        adj = _a.astype(jnp.int32)
        return (x, adj)
    x, adj = _rec_inputs()

    def _L0_gnn_setup():
        import jax, jax.numpy as jnp
        import numpy as np
        N = 4096
        D_IN = 128
        D_OUT = 128
        NEG_INF = -9000000000000000.0
        key = jax.random.key(seed)
        k1, k2, k3, k4 = jax.random.split(key, 4)
        node_features = jax.random.normal(k1, (N, D_IN), dtype=jnp.float32)
        adjacency_matrix = jax.random.randint(k2, (N, N), 0, 2, dtype=jnp.int32)
        W = jax.random.normal(k3, (D_OUT, D_IN), dtype=jnp.float32) / np.sqrt(D_IN)
        b_W = jnp.zeros((D_OUT,), dtype=jnp.float32)
        a_vec = jax.random.normal(k4, (2 * D_OUT,), dtype=jnp.float32) / np.sqrt(2 * D_OUT)
        b_a = jnp.zeros((1,), dtype=jnp.float32)
        return {'node_features': node_features, 'adjacency_matrix': adjacency_matrix, 'W': W, 'b_W': b_W, 'a_vec': a_vec, 'b_a': b_a}
    _L0_gnn_all = _L0_gnn_setup()
    _L0_gnn_in = {k: v for k, v in _L0_gnn_all.items() if k in ('W', 'b_W', 'a_vec', 'b_a')}
    del _L0_gnn_all
    return {'x': x, 'adj': adj, 'L0_gnn_W': _L0_gnn_in['W'], 'L0_gnn_b_W': _L0_gnn_in['b_W'], 'L0_gnn_a_vec': _L0_gnn_in['a_vec'], 'L0_gnn_b_a': _L0_gnn_in['b_a']}

def reference(x, adj, L0_gnn_W, L0_gnn_b_W, L0_gnn_a_vec, L0_gnn_b_a):
    import jax
    import jax.numpy as jnp

    def _L0_gnn_ref(node_features, adjacency_matrix, W, b_W, a_vec, b_a):
        import jax, jax.numpy as jnp
        import numpy as np
        N = 4096
        D_IN = 128
        D_OUT = 128
        NEG_INF = -9000000000000000.0
        h = node_features @ W.T + b_W
        a1, a2 = (a_vec[:D_OUT], a_vec[D_OUT:])
        e = (h @ a1)[:, None] + (h @ a2)[None, :] + b_a[0]
        e = jnp.where(e > 0, e, 0.2 * e)
        scores = jnp.where(adjacency_matrix > 0, e, jnp.float32(NEG_INF))
        attention = jax.nn.softmax(scores, axis=1)
        h_prime = attention @ h
        return h_prime
    x = _layernorm(x + _L0_gnn_ref(x, adj, L0_gnn_W, L0_gnn_b_W, L0_gnn_a_vec, L0_gnn_b_a), axis=-1)
    return x

_drawn_inputs = setup_inputs


def setup_inputs(seed=0):
    import zlib

    import numpy as np

    out = dict(_drawn_inputs(seed))
    spreads = {'L0_gnn_b_W': (0.0, 0.1)}
    factors = {}
    for name, (base, spread) in spreads.items():
        noise = np.random.default_rng([zlib.crc32(name.encode()), seed]).standard_normal(out[name].shape)
        drawn = base * np.exp(spread * noise) if base else spread * noise
        out[name] = jnp.asarray(drawn.astype(out[name].dtype))
    for name, factor in factors.items():
        out[name] = (out[name] * factor).astype(out[name].dtype)
    return out
```

```python
import concourse.bass as bass
from concourse import mybir
from concourse.alu_op_type import AluOpType as ALU
from contextlib import ExitStack


P = 128
F32, F16, U8, U32, I8 = (mybir.dt.float32, mybir.dt.float16, mybir.dt.uint8, mybir.dt.uint32, mybir.dt.int8)
I32, F8 = mybir.dt.int32, mybir.dt.float8e4
ACT = mybir.ActivationFunctionType
AX = mybir.AxisListType
RMAX = bass.bass_isa.ReduceOp.max

D = 128
Q = 4
SLOPE = 0.2
EPS = 1e-5
EDGE = 0x78
POS, NEG = 0x38, 0x40
NEG_SCALE = 0.5
WORD = 0x01010101
W_TOP = 2.0 ** 15
TINY = 1e-30
TAIL_STEPS = 7


def gat_kernel(nc, x, adj, w_in, b_w, a_vec, b_a, out, s_lin):
    N = x.shape[0]
    QC = N // Q
    NB = QC // P
    KT = NB * 4
    BLOCKS = N // P
    PAIRS = BLOCKS // 2
    SLAB = 2
    SLABS = 2
    SC = SLAB * QC
    SW = SC // 4
    RING = 4
    DA = D + 1
    DS = D + 2
    MV = 2 * DA

    ctx = ExitStack()
    with ctx:
        def sb(name, shape, dt):
            return ctx.enter_context(nc.sbuf_tensor(name, shape, dt))

        def sem(name):
            return ctx.enter_context(nc.semaphore(name))

        adj_ring = sb("adj_ring", [P, RING, SC], I32)
        work = sb("work", [P, 4 * KT * P // 4 + 2 * SW], U32)
        w_parts = sb("w_parts", [P, KT, 2, MV], F16)
        s2_row = sb("s2_row", [P, QC], F32)
        edge = sb("edge", [P, 2, SC], U8)
        sign = sb("sign", [P, 2, SC], I8)
        scaled = sb("scaled", [P, 2, MV], F32)
        both = sb("both", [P, 2, MV], F32)
        num = sb("num", [P, 2, DA], F32)
        x_blk = sb("x_blk", [P, 2, D], F32)
        y_blk = sb("y_blk", [P, 2, D], F32)
        o_blk = sb("o_blk", [P, 2, D], F32)
        h_mean = sb("h_mean", [P, D], F32)
        rden = sb("rden", [P, 2, 4], F32)
        stats = sb("stats", [P, 2, 6], F32)
        mv = sb("mv", [P, 2, 4], F32)
        s1_stripe = sb("s1_stripe", [P, N // 32], F32)
        u_row = sb("u_row", [P, 8, BLOCKS], F32)
        ident = sb("ident", [P, P], F32)
        ones = sb("ones", [P, P], F32)
        a_col = sb("a_col", [P, 2], F32)
        bw_col = sb("bw_col", [P, 1], F32)
        ba_sb = sb("ba_sb", [1, 1], F32)
        tops = sb("tops", [P, 20], F32)
        top_all = sb("top_all", [P, 8], F32)
        eps_col = sb("eps_col", [P, 1], F32)
        psum = ctx.enter_context(nc.psum_tensor("psum", [P, 8, 512], F32))

        early = sign[:, :, :].bitcast(F32).rearrange("p u n -> p (u n)")
        sizes = [0, D, DS, DS, DS, 2 * KT, 6 * KT, N // P, N // 32, P]
        starts = [sum(sizes[:n + 1]) for n in range(len(sizes))]
        w_sb, wt, bias_row, bias_all, s_col, v_col, s1_lin, s1_rep, s1_blk = (early[:, a:b] for a, b in zip(starts, starts[1:]))
        bias_row, s1_blk = bias_row[0:1], s1_blk[0:BLOCKS]
        s_col = s_col.rearrange("p (w t) -> p w t", w=2)
        v_col = v_col.rearrange("p (w t) -> p w t", w=6)
        s1_lin = s1_lin.rearrange("p (h i) -> p h i", h=2)
        s1_rep = s1_rep.rearrange("p (h q i) -> p h q i", h=2, q=Q)
        masks = work[:, 0:4 * KT * P // 4].rearrange("p (u m b s i) -> p u m b s i", u=2, m=2, b=NB, s=4)
        masks8 = work[:, 0:4 * KT * P // 4].bitcast(F8).rearrange("p (u m n) -> p u m n", u=2, m=2)
        turned = work[:, 4 * KT * P // 4:4 * KT * P // 4 + 2 * SW].rearrange("p (u w) -> p u w", u=2)
        hs = work[:, 0:KT * DS].bitcast(F32).rearrange("p (t d) -> p t d", d=DS)
        x_all = adj_ring[:, 2:4, :].bitcast(F32).rearrange("p u n -> p (u n)").rearrange("p (b k d) -> p b k d", b=NB, k=4)
        xt = adj_ring[:, 1, :].bitcast(F32).rearrange("p (u n) -> p u n", u=SC // 512)
        edge32 = edge[:, :, :].bitcast(U32)
        sign32 = sign[:, :, :].bitcast(U32)
        acc = lambda u, m: psum[:, 2 * u + m, 0:MV]
        ps_xt = lambda g: psum[:, g % 2, :]
        ps_h = lambda g: psum[:, 2 + 2 * (g % 2):4 + 2 * (g % 2), :].rearrange("p a (b n) -> p (a b) n", b=2)
        ps_small = psum[:, 6, :]
        ps_mean = psum[:, 7, 0:D]

        adj_in = [sem(f"adj_in{r}") for r in range(RING)]
        x_in, wts_in, x_blk_in, out_done = sem("x_in"), sem("wts_in"), [sem(f"x_blk_in{u}") for u in range(2)], [sem(f"out_done{u}") for u in range(2)]
        s_out, s2_row_in, s1_lin_in = sem("s_out"), sem("s2_row_in"), sem("s1_lin_in")
        consts, ident0 = sem("consts"), sem("ident0")
        wt_ps, wt_sb, bias_ps, bias_sb = sem("wt_ps"), sem("wt_sb"), sem("bias_ps"), sem("bias_sb")
        xt_ps, xt_sb, h_ps, h_sb = sem("xt_ps"), sem("xt_sb"), sem("h_ps"), sem("h_sb")
        vchain, top_red, aug_set, s_copied, mean_ps, mean_sb = sem("vchain"), sem("top_red"), sem("aug_set"), sem("s_copied"), sem("mean_ps"), sem("mean_sb")
        v_arg, v_exp, v_scaled, w_hi, w_lo = sem("v_arg"), sem("v_exp"), sem("v_scaled"), sem("w_hi"), sem("w_lo")
        s1_spread, s1_ps, s1_set, u_arg, u_exp, u_set = sem("s1_spread"), sem("s1_ps"), sem("s1_set"), sem("u_arg"), sem("u_exp"), sem("u_set")
        edge_done, sign_done, code_done, turn_done, mask_done = sem("edge_done"), sem("sign_done"), sem("code_done"), sem("turn_done"), sem("mask_done")
        acc_done, scaled_done, both_done, num_done, y_done, std_done, norm_done = (sem(n) for n in ("acc_done", "scaled_done", "both_done", "num_done", "y_done", "std_done", "norm_done"))
        h_top, rstd_done, tail = sem("h_top"), sem("rstd_done"), sem("tail")

        carried = {e: sem(f"carried_{n}") for n, e in (("pool", nc.gpsimd.engine), ("pe", nc.tensor.engine), ("dve", nc.vector.engine))}
        block = ctx.enter_context(nc.Block())

        x_tiles = x.rearrange("(q b c k) d -> q c b (k d)", q=Q, b=NB, c=32)
        adj_rows = adj.rearrange("(r s i) (q n) -> q i r s n", s=SLAB, i=32, q=Q)
        s_tiles = s_lin.rearrange("w (q b c k) -> w q c b k", q=Q, b=NB, c=32)

        def quad(q):
            return slice(32 * q, 32 * q + 32)

        def at_least(eng, semaphore, value, first):
            if not first or value > 0:
                eng.wait_ge(semaphore, value)

        def carry(eng):
            eng.sem_inc(carried[eng.engine], 1)

        @block.sync
        def _(sp):
            def slab_in(pair, i, first):
                slab = pair * 4 + i
                if not first:
                    sp.wait_ge(edge_done, slab - RING + 1)
                for q in range(Q):
                    sp.dma_start(adj_ring[quad(q), i, :].rearrange("p (s n) -> p s n", s=SLAB),
                                 adj_rows[q, :, bass.ds(slab, 1), :, :].rearrange("i r s n -> i (r s) n")).then_inc(adj_in[i], 16)

            for q in range(Q):
                sp.dma_start(x_all[quad(q)].rearrange("p b k d -> p b (k d)"), x_tiles[q]).then_inc(x_in, 16)
            slab_in(0, 0, True)
            sp.wait_ge(h_sb, NB)
            for i in range(1, 4):
                slab_in(0, i, True)
            with sp.Fori(1, PAIRS) as pair:
                for i in range(4):
                    slab_in(pair, i, False)

        @block.gpsimd
        def _(pool):
            nc.gpsimd.memset(ident[:], 0.0).then_inc(ident0, 1)
            nc.gpsimd.memset(ones[:], 1.0).then_inc(consts, 1)
            nc.gpsimd.memset(eps_col[:], EPS).then_inc(consts, 1)
            pool.wait_ge(ident0, 1)
            nc.gpsimd.affine_select(out=ident[:], in_=ident[:], compare_op=ALU.not_equal, fill=1.0, base=0,
                                    pattern=[[-1, P]], channel_multiplier=1).then_inc(consts, 1)
            pool.wait_ge(vchain, 3)
            nc.gpsimd.partition_all_reduce(top_all[:, 0:3], tops[:, 0:3], P, RMAX).then_inc(top_red, 1)

            def sums(blk, u, first):
                pool.wait_ge(both_done, blk + 1)
                nc.gpsimd.tensor_tensor(num[:, u, :], both[:, u, 0:DA], both[:, u, DA:MV], ALU.add).then_inc(num_done, 1)

            def norm(blk, u, first):
                pool.wait_ge(rstd_done, blk + 1)
                carry(pool)
                nc.gpsimd.tensor_scalar(o_blk[:, u, :], y_blk[:, u, :], mv[:, u, 0:1], mv[:, u, 3:4],
                                        ALU.subtract, ALU.mult).then_inc(norm_done, 1)

            def store(pair, u, first):
                blk = pair * 2 + u
                pool.wait_ge(norm_done, blk + 1)
                pool.dma_start(out[bass.ds(blk * P, P), :], o_blk[:, u, :]).then_inc(out_done[u], 16)

            def both_blocks(pair, first):
                for u in range(2):
                    sums(pair * 2 + u, u, first)
                    if not first:
                        pool.wait_ge(out_done[u], pair * 16)
                    norm(pair * 2 + u, u, first)
                    store(pair, u, first)

            both_blocks(0, True)
            with pool.Fori(1, PAIRS) as pair:
                both_blocks(pair, False)
            for u in range(2):
                pool.wait_ge(out_done[u], PAIRS * 16)

        @block.scalar
        def _(act):
            act.dma_start(w_sb[:], w_in).then_inc(wts_in, 16)
            act.dma_start(a_col[:], a_vec.rearrange("(c o) -> o c", c=2), allow_slow_non_contiguous=True).then_inc(wts_in, 16)
            act.dma_start(bw_col[:], b_w.rearrange("(o c) -> o c", c=1), allow_slow_non_contiguous=True).then_inc(wts_in, 16)
            act.dma_start(bias_row[0:1, 0:D], b_w.rearrange("(c o) -> c o", c=1)).then_inc(wts_in, 16)
            act.dma_start(ba_sb[:], b_a.rearrange("(c o) -> c o", c=1)).then_inc(wts_in, 16)
            for g in range(NB):
                act.wait_ge(xt_ps, g + 1)
                if g >= 2:
                    act.wait_ge(h_ps, g - 1)
                nc.scalar.copy(xt[:, g % 2, :], ps_xt(g)).then_inc(xt_sb, 1)
            act.wait_ge(s_copied, 1)
            for w in range(2):
                for q in range(Q):
                    act.dma_start(s_tiles[w, q], s_col[quad(q), w, :].rearrange("p (b k) -> p b k", k=4)).then_inc(s_out, 16)
            act.wait_ge(s_out, 2 * Q * 16)
            for q in range(Q):
                act.dma_start(s2_row[quad(q), :], s_lin[1:2, q * QC:(q + 1) * QC].to_broadcast([32, QC])).then_inc(s2_row_in, 16)
            act.dma_start(s1_lin[:], s_lin[0].rearrange("(h s i) -> s h i", h=2, i=32)).then_inc(s1_lin_in, 16)
            act.dma_start(s1_blk[:], s_lin[0].rearrange("(n p) -> n p", p=P)).then_inc(s1_lin_in, 16)
            act.wait_ge(v_arg, 1)
            nc.scalar.activation(v_col[:, 2, :], v_col[:, 0, :], ACT.Exp).then_inc(v_exp, 1)
            nc.scalar.activation(v_col[:, 3, :], v_col[:, 0, :], ACT.Exp, scale=SLOPE).then_inc(v_exp, 1)
            act.wait_ge(aug_set, 1)
            act.wait_ge(v_scaled, 2)
            for t in range(KT):
                for m in range(2):
                    nc.scalar.mul(w_parts[:, t, m, 0:DA], hs[:, t, 0:DA], v_col[:, 4 + m, t:t + 1]).then_inc(w_hi, 1)
            act.wait_ge(mean_ps, 1)
            nc.scalar.mul(h_mean[:], ps_mean, 1.0 / N).then_inc(mean_sb, 1)
            act.wait_ge(u_arg, 1)
            nc.scalar.activation(u_row[:, 4:6, :], u_row[:, 2:4, :], ACT.Exp).then_inc(u_exp, 1)
            act.wait_ge(s2_row_in, Q * 16)
            act.wait_ge(s1_set, 1)

            def signs(blk, u, sl, first):
                slab = blk * SLABS + sl
                at_least(act, code_done, slab - 1, first)
                for s in range(SLAB):
                    col = slab * SLAB + s
                    nc.scalar.activation(sign[:, sl, s * QC:(s + 1) * QC], s2_row[:], ACT.Sign,
                                         bias=s1_stripe[:, bass.ds(col, 1)]).then_inc(sign_done, 1)

            def scale(blk, u):
                act.wait_ge(acc_done, blk + 1)
                nc.scalar.mul(scaled[:, u, :], acc(u, 0), u_row[:, 4, bass.ds(blk, 1)]).then_inc(scaled_done, 1)

            def load_x(blk, u, first):
                if not first:
                    act.wait_ge(y_done, blk)
                act.dma_start(x_blk[:, u, :], x[bass.ds(blk * P, P), :]).then_inc(x_blk_in[u], 16)

            def std(blk, u):
                act.wait_ge(y_done, blk + 2)
                nc.scalar.activation(mv[:, u, 2:3], mv[:, u, 1:2], ACT.Sqrt, bias=eps_col[:]).then_inc(std_done, 1)

            def iteration(pair, first):
                for u in range(2):
                    blk = pair * 2 + u
                    signs(blk, u, 0, first)
                    if not first:
                        scale(blk - 2, u)
                    if not first:
                        load_x(blk - 1, 1 - u, False)
                    elif u == 1:
                        load_x(0, 0, True)
                    signs(blk, u, 1, first)
                    if not first:
                        std(blk - 2, u)

            iteration(0, True)
            with act.Fori(1, PAIRS) as pair:
                iteration(pair, False)
            load_x(BLOCKS - 1, 1, False)
            for u in range(2):
                scale(BLOCKS - 2 + u, u)
                std(BLOCKS - 2 + u, u)

        @block.tensor
        def _(pe):
            pe.wait_ge(consts, 3)
            pe.wait_ge(wts_in, 5 * 16)
            nc.tensor.transpose(ps_small[:, 0:D], w_sb[:], ident[:]).then_inc(wt_ps, 1)
            nc.tensor.matmul(ps_mean[:, 0:2], w_sb[:], a_col[:], start=True, stop=True).then_inc(wt_ps, 1)
            nc.tensor.matmul(ps_mean[0:1, 64:66], bw_col[:], a_col[:], start=True, stop=True).then_inc(wt_ps, 1)
            pe.wait_ge(bias_sb, 1)
            pe.wait_ge(wt_sb, 3)
            nc.tensor.matmul(ps_small[:, 256:256 + DS], ones[0:1, :], bias_row[:], start=True, stop=True).then_inc(bias_ps, 1)
            pe.wait_ge(x_in, Q * 16)

            def turn_x(g):
                if g >= 2:
                    pe.wait_ge(xt_sb, g - 1)
                for k in range(4):
                    last = nc.tensor.transpose(ps_xt(g)[:, k * P:(k + 1) * P], x_all[:, g, k, :], ident[:])
                last.then_inc(xt_ps, 1)

            turn_x(0)
            for g in range(NB):
                if g + 1 < NB:
                    turn_x(g + 1)
                pe.wait_ge(xt_sb, g + 1)
                if g >= 2:
                    pe.wait_ge(h_sb, g - 1)
                for k in range(4):
                    last = nc.tensor.matmul(ps_h(g)[:, k, 0:DS], xt[:, g % 2, k * P:(k + 1) * P], wt[:], start=True, stop=True)
                last.then_inc(h_ps, 1)
            pe.wait_ge(h_sb, NB)
            for t in range(KT):
                last = nc.tensor.matmul(ps_mean, ones[:], hs[:, t, 0:D], start=(t == 0), stop=(t == KT - 1))
            last.then_inc(mean_ps, 1)
            pe.wait_ge(s1_spread, 1)
            for half in range(2):
                last = nc.tensor.transpose(ps_small[:, half * P:(half + 1) * P],
                                           s1_rep[:, half].rearrange("s q i -> s (q i)"), ident[:])
            nc.tensor.transpose(ps_small[:, 2 * P:2 * P + BLOCKS], s1_blk[:], ident[0:BLOCKS, 0:BLOCKS]).then_inc(s1_ps, 1)
            pe.wait_ge(w_lo, 2 * KT)
            pe.wait_ge(u_set, 1)

            def block_sums(pair, u, first):
                blk = pair * 2 + u
                if not first:
                    pe.wait_ge(both_done, blk - 1)
                pe.wait_ge(mask_done, 2 * SLABS * (blk + 1))
                carry(pe)
                for t in range(KT):
                    b, k = divmod(t, 4)
                    for m in range(2):
                        o = b * 4 * P + k
                        last = nc.tensor.matmul(acc(u, m), masks8[:, u, m, o:o + 4 * (P - 1) + 1:4], w_parts[:, t, m, :],
                                                start=(t == 0), stop=(t == KT - 1))
                last.then_inc(acc_done, 1)

            for u in range(2):
                block_sums(0, u, True)
            with pe.Fori(1, PAIRS) as pair:
                for u in range(2):
                    block_sums(pair, u, False)

        @block.vector
        def _(dve):
            dve.wait_ge(wt_ps, 3)
            nc.vector.tensor_copy(wt[:, 0:D], ps_small[:, 0:D]).then_inc(wt_sb, 1)
            nc.vector.tensor_copy(wt[:, D:DS], ps_mean[:, 0:2]).then_inc(wt_sb, 1)
            nc.vector.tensor_scalar(bias_row[0:1, D:D + 1], ps_mean[0:1, 64:65], ba_sb[0:1, 0:1], None, ALU.add).then_inc(bias_sb, 1)
            nc.vector.tensor_copy(bias_row[0:1, D + 1:DS], ps_mean[0:1, 65:66]).then_inc(wt_sb, 1)
            dve.wait_ge(bias_ps, 1)
            nc.vector.tensor_copy(bias_all[:], ps_small[:, 256:256 + DS]).then_inc(bias_sb, 1)
            dve.wait_ge(bias_sb, 2)
            for g in range(NB):
                dve.wait_ge(h_ps, g + 1)
                nc.vector.tensor_tensor(hs[:, 4 * g:4 * g + 4, :], ps_h(g)[:, :, 0:DS],
                                        bias_all[:].rearrange("p (a d) -> p a d", a=1).to_broadcast([P, 4, DS]), ALU.add).then_inc(h_sb, 1)
                if g >= 1:
                    dve.wait_ge(h_sb, g)
                    nc.vector.tensor_reduce(tops[:, 4 + g - 1:4 + g], hs[:, 4 * g - 4:4 * g, 0:D], AX.XY, ALU.max,
                                            apply_absolute_value=True).then_inc(h_top, 1)
            dve.wait_ge(h_sb, NB)
            nc.vector.tensor_copy(s_col[:].rearrange("p w t -> p t w"), hs[:, :, D:DS]).then_inc(s_copied, 1)
            nc.vector.tensor_reduce(tops[:, 4 + NB - 1:4 + NB], hs[:, KT - 4:KT, 0:D], AX.XY, ALU.max,
                                    apply_absolute_value=True).then_inc(h_top, 1)
            dve.wait_ge(s_copied, 1)
            nc.vector.tensor_reduce(tops[:, 0:1], s_col[:, 1, :], AX.X, ALU.max).then_inc(vchain, 1)
            nc.vector.tensor_reduce(tops[:, 1:2], s_col[:, 1, :], AX.X, ALU.min, negate=True).then_inc(vchain, 1)
            dve.wait_ge(h_top, NB)
            nc.vector.tensor_reduce(tops[:, 2:3], tops[:, 4:4 + NB], AX.X, ALU.max).then_inc(vchain, 1)
            dve.wait_ge(top_red, 1)
            nc.vector.tensor_scalar(v_col[:, 0, :], s_col[:, 1, :], top_all[:, 0:1], None, ALU.subtract).then_inc(v_arg, 1)
            nc.vector.tensor_scalar(top_all[:, 3:4], top_all[:, 2:3], TINY, None, ALU.max).then_inc(vchain, 1)
            dve.wait_ge(vchain, 4)
            nc.vector.reciprocal(top_all[:, 4:5], top_all[:, 3:4]).then_inc(vchain, 1)
            nc.vector.tensor_copy(hs[:, :, D], top_all[:, 3:4].to_broadcast([P, KT])).then_inc(aug_set, 1)
            dve.wait_ge(vchain, 5)
            dve.wait_ge(v_exp, 2)
            for m in range(2):
                nc.vector.tensor_scalar(v_col[:, 4 + m, :], v_col[:, 2 + m, :], top_all[:, 4:5], W_TOP, ALU.mult, ALU.mult).then_inc(v_scaled, 1)
            dve.wait_ge(s1_lin_in, 32)
            nc.vector.tensor_copy(s1_rep[:], s1_lin[:].rearrange("p h (a i) -> p h a i", a=1).to_broadcast([P, 2, Q, 32])).then_inc(s1_spread, 1)
            dve.wait_ge(v_scaled, 2)
            dve.wait_ge(aug_set, 1)
            for t in range(KT):
                for m in range(2):
                    dve.wait_ge(w_hi, 2 * t + m + 1)
                    nc.vector.scalar_tensor_tensor(w_parts[:, t, m, DA:MV], hs[:, t, 0:DA], v_col[:, 4 + m, t:t + 1],
                                                   w_parts[:, t, m, 0:DA], ALU.mult, ALU.subtract).then_inc(w_lo, 1)
            dve.wait_ge(s1_ps, 1)
            nc.vector.tensor_copy(s1_stripe[:], ps_small[:, 0:2 * P]).then_inc(s1_set, 1)
            nc.vector.tensor_scalar(u_row[:, 0, :], ps_small[:, 2 * P:2 * P + BLOCKS], top_all[:, 0:1], None, ALU.add).then_inc(vchain, 1)
            dve.wait_ge(vchain, 6)
            nc.vector.scalar_tensor_tensor(u_row[:, 1, :], u_row[:, 0, :], SLOPE, u_row[:, 0, :], ALU.mult, ALU.max).then_inc(vchain, 1)
            dve.wait_ge(vchain, 7)
            nc.vector.tensor_tensor(u_row[:, 2, :], u_row[:, 0, :], u_row[:, 1, :], ALU.subtract).then_inc(vchain, 1)
            nc.vector.scalar_tensor_tensor(u_row[:, 3, :], u_row[:, 0, :], SLOPE, u_row[:, 1, :], ALU.mult, ALU.subtract).then_inc(vchain, 1)
            dve.wait_ge(vchain, 9)
            nc.vector.engine_nop().then_inc(u_arg, 1)
            nc.vector.engine_nop().then_inc(y_done, 1)
            dve.wait_ge(u_exp, 1)
            nc.vector.tensor_scalar(u_row[:, 6, :], u_row[:, 5, :], NEG_SCALE, None, ALU.mult).then_inc(u_set, 1)
            dve.wait_ge(u_set, 1)
            dve.wait_ge(mean_sb, 1)
            dve.wait_ge(w_lo, 2 * KT)

            def slab_codes(pair, u, sl, first):
                blk = pair * 2 + u
                slab = blk * SLABS + sl
                slot = u * SLABS + sl
                dve.wait_ge(adj_in[slot], (pair + 1) * Q * 16)
                nc.vector.tensor_scalar(edge[:, sl, :], adj_ring[:, slot, :], 0.0, float(EDGE), ALU.is_gt, ALU.mult).then_inc(edge_done, 1)
                dve.wait_ge(sign_done, SLAB * (slab + 1))
                dve.wait_ge(edge_done, slab + 1)
                nc.vector.scalar_tensor_tensor(edge32[:, sl, :], sign32[:, sl, :], POS * WORD, edge32[:, sl, :],
                                               ALU.bitwise_xor, ALU.bitwise_and).then_inc(code_done, 1)
                dve.wait_ge(code_done, slab + 1)
                nc.vector.transpose(turned[:, sl, :], edge32[:, sl, :]).then_inc(turn_done, 1)

            def slab_masks(pair, u, sl, first):
                blk = pair * 2 + u
                slab = blk * SLABS + sl
                dve.wait_ge(turn_done, slab + 1)
                if not first:
                    dve.wait_ge(acc_done, blk - 1)
                src = turned[:, sl, :].rearrange("p (s b i) -> p b s i", s=SLAB, b=NB)
                for m, byte in enumerate((POS, NEG)):
                    last = nc.vector.tensor_scalar(masks[:, u, m, :, sl * SLAB:(sl + 1) * SLAB, :], src, byte * WORD, None, ALU.bitwise_and)
                    last.then_inc(mask_done, 1)

            def combine(blk, u):
                dve.wait_ge(scaled_done, blk + 1)
                nc.vector.scalar_tensor_tensor(both[:, u, :], acc(u, 1), u_row[:, 6, bass.ds(blk, 1)], scaled[:, u, :],
                                               ALU.mult, ALU.add).then_inc(both_done, 1)

            def finish(pair, u):
                blk = pair * 2 + u
                n = [0]

                def step(ins):
                    n[0] += 1
                    ins.then_inc(tail, 1)
                    dve.wait_ge(tail, blk * TAIL_STEPS + n[0])

                dve.wait_ge(num_done, blk + 1)
                step(nc.vector.tensor_scalar(rden[:, u, 0:1], num[:, u, D:DA], TINY, None, ALU.max))
                step(nc.vector.tensor_scalar(rden[:, u, 1:2], num[:, u, D:DA], 0.0, None, ALU.is_equal))
                step(nc.vector.reciprocal(rden[:, u, 2:3], rden[:, u, 0:1]))
                step(nc.vector.tensor_scalar(rden[:, u, 3:4], rden[:, u, 2:3], top_all[:, 3:4], None, ALU.mult))
                dve.wait_ge(x_blk_in[u], (pair + 1) * 16)
                step(nc.vector.scalar_tensor_tensor(y_blk[:, u, :], h_mean[:], rden[:, u, 1:2], x_blk[:, u, :], ALU.mult, ALU.add))
                step(nc.vector.scalar_tensor_tensor(y_blk[:, u, :], num[:, u, 0:D], rden[:, u, 3:4], y_blk[:, u, :], ALU.mult, ALU.add))
                step(nc.vector.bn_stats(stats[:, u, :], y_blk[:, u, :]))
                carry(dve)
                nc.vector.bn_aggr(mv[:, u, 0:2], stats[:, u, :]).then_inc(y_done, 1)

            def inverse_std(blk, u):
                dve.wait_ge(std_done, blk + 1)
                nc.vector.reciprocal(mv[:, u, 3:4], mv[:, u, 2:3]).then_inc(rstd_done, 1)

            def iteration(pair, first):
                for u in range(2):
                    slab_codes(pair, u, 0, first)
                    slab_masks(pair, u, 0, first)
                    if not first:
                        combine(pair * 2 + u - 2, u)
                    slab_codes(pair, u, 1, first)
                    if not first:
                        finish(pair - 1, u)
                    slab_masks(pair, u, 1, first)
                    if not first:
                        inverse_std(pair * 2 + u - 2, u)

            iteration(0, True)
            with dve.Fori(1, PAIRS) as pair:
                iteration(pair, False)
            for u in range(2):
                combine(BLOCKS - 2 + u, u)
                finish(PAIRS - 1, u)
                inverse_std(BLOCKS - 2 + u, u)


_INS = ["x", "adj", "L0_gnn_W", "L0_gnn_b_W", "L0_gnn_a_vec", "L0_gnn_b_a"]


def kernel(**inputs):
    import numpy as _np
    import concourse.bacc as _bacc
    from concourse import mybir as _mybir
    from concourse.bass_utils import run_bass_kernel_spmd as _run

    nc = _bacc.Bacc("TRN2", target_bir_lowering=False, num_devices=1)
    arrays, args = {}, []
    for name in _INS:
        a = _np.ascontiguousarray(inputs[name])
        arrays[f"in_{name}"] = a
        args.append(nc.dram_tensor(f"in_{name}", a.shape, _mybir.dt.from_np(a.dtype), kind="ExternalInput").ap())
    n, d = inputs["x"].shape
    out = nc.dram_tensor("out_0", (n, d), _mybir.dt.float32, kind="ExternalOutput").ap()
    s_lin = nc.dram_tensor("s_lin", (2, n), _mybir.dt.float32, kind="Internal").ap()
    gat_kernel(nc, *args, out, s_lin)
    r = _run(nc, [arrays], core_ids=[0])
    return r.results[0]["out_0"]
```

```python
import concourse.bass as bass
from concourse import mybir
from concourse.alu_op_type import AluOpType as ALU
from contextlib import ExitStack


P = 128
F32, F16, U8, U32, I8 = (mybir.dt.float32, mybir.dt.float16, mybir.dt.uint8, mybir.dt.uint32, mybir.dt.int8)
I32, F8 = mybir.dt.int32, mybir.dt.float8e4
ACT = mybir.ActivationFunctionType
AX = mybir.AxisListType
RMAX = bass.bass_isa.ReduceOp.max

D = 128
Q = 4
SLOPE = 0.2
HEAD = 12
EPS = 1e-5
EDGE = 0x78
POS, NEG = 0x38, 0x40
NEG_SCALE = 0.5
WORD = 0x01010101
W_TOP = 2.0 ** 15
TINY = 1e-30
POOL_STEPS = 5
TAIL_STEPS = 2


def gat_kernel(nc, x, adj, w_in, b_w, a_vec, b_a, out, s_lin):
    N = x.shape[0]
    QC = N // Q
    NB = QC // P
    KT = NB * 4
    BLOCKS = N // P
    PAIRS = BLOCKS // 2
    SLAB = 2
    SLABS = 2
    SC = SLAB * QC
    SW = SC // 4
    RING = 4
    DA = D + 1
    DS = D + 2
    MV = 2 * DA

    ctx = ExitStack()
    with ctx:
        def sb(name, shape, dt):
            return ctx.enter_context(nc.sbuf_tensor(name, shape, dt))

        def sem(name):
            return ctx.enter_context(nc.semaphore(name))

        adj_ring = sb("adj_ring", [P, RING, SC], I32)
        mask_words = sb("mask_words", [P, KT * P], U32)
        turned = sb("turned", [P, 2, SW], U32)
        w_parts = sb("w_parts", [P, KT, 2, MV], F16)
        s2_row = sb("s2_row", [P, QC], F32)
        edge = sb("edge", [P, 2, SC], U8)
        sign = sb("sign", [P, 2, SC], I8)
        scaled = sb("scaled", [P, 2, MV], F32)
        both = sb("both", [P, 2, MV], F32)
        num = sb("num", [P, 2, D], F32)
        x_blk = sb("x_blk", [P, 2, D], F32)
        y_blk = sb("y_blk", [P, 2, D], F32)
        o_blk = sb("o_blk", [P, 2, D], F32)
        h_mean = sb("h_mean", [P, D], F32)
        den = sb("den", [P, 2, 4], F32)
        rest = sb("rest", [P, 2, D], F32)
        minus_half = sb("minus_half", [P, 1], F32)
        stats = sb("stats", [P, 2, 6], F32)
        mv = sb("mv", [P, 2, 4], F32)
        s1_stripe = sb("s1_stripe", [P, N // 32], F32)
        u_row = sb("u_row", [P, 8, BLOCKS], F32)
        a_col = sb("a_col", [P, 2], F32)
        bw_col = sb("bw_col", [P, 1], F32)
        ba_sb = sb("ba_sb", [1, 1], F32)
        v_col = sb("v_col", [P, 6, KT], F32)
        tops = sb("tops", [P, 20], F32)
        top_all = sb("top_all", [P, 8], F32)
        
        psum = ctx.enter_context(nc.psum_tensor("psum", [P, 8, 512], F32))

        early = sign[:, :, :].bitcast(F32).rearrange("p u n -> p (u n)")
        sizes = [0, D, DS, DS, DS, 2 * KT, N // P, N // 32, P, P, P]
        starts = [sum(sizes[:n + 1]) for n in range(len(sizes))]
        w_sb, wt, bias_row, bias_all, s_col, s1_lin, s1_rep, s1_blk, ident, ones = (early[:, a:b] for a, b in zip(starts, starts[1:]))
        bias_row, s1_blk = bias_row[0:1], s1_blk[0:BLOCKS]
        s_col = s_col.rearrange("p (w t) -> p w t", w=2)
        s1_lin = s1_lin.rearrange("p (h i) -> p h i", h=2)
        s1_rep = s1_rep.rearrange("p (h q i) -> p h q i", h=2, q=Q)
        masks = mask_words[:, :].rearrange("p (u m b s i) -> p u m b s i", u=2, m=2, b=NB, s=4)
        masks8 = mask_words[:, :].bitcast(F8).rearrange("p (u m n) -> p u m n", u=2, m=2)
        x_all = adj_ring[:, 2:4, :].bitcast(F32).rearrange("p u n -> p (u n)").rearrange("p (b k d) -> p b k d", b=NB, k=4)
        hs = x_all.rearrange("p b k d -> p (b k) d")
        xt = adj_ring[:, 1, :].bitcast(F32).rearrange("p (u n) -> p u n", u=SC // 512)
        edge32 = edge[:, :, :].bitcast(U32)
        sign32 = sign[:, :, :].bitcast(U32)
        acc = lambda u, m: psum[:, 2 * u + m, 0:MV]
        ps_xt = lambda g: psum[:, g % 2, :]
        ps_h = lambda g: psum[:, 2 + 2 * (g % 2):4 + 2 * (g % 2), :].rearrange("p a (b n) -> p (a b) n", b=2)
        ps_small = psum[:, 6, :]
        ps_mean = psum[:, 7, 0:D]

        adj_in = [sem(f"adj_in{r}") for r in range(RING)]
        x_in, wts_in, x_blk_in, out_done = sem("x_in"), sem("wts_in"), [sem(f"x_blk_in{u}") for u in range(2)], [sem(f"out_done{u}") for u in range(2)]
        s_out, s2_row_in, s1_lin_in = sem("s_out"), sem("s2_row_in"), sem("s1_lin_in")
        consts, ident0 = sem("consts"), sem("ident0")
        pool_step, den_done, rest_done, rden_done = sem("pool_step"), sem("den_done"), sem("rest_done"), sem("rden_done")
        wt_ps, wt_sb, bias_ps, bias_sb = sem("wt_ps"), sem("wt_sb"), sem("bias_ps"), sem("bias_sb")
        xt_ps, xt_sb, h_ps, h_sb, s_sb = sem("xt_ps"), sem("xt_sb"), sem("h_ps"), sem("h_sb"), sem("s_sb")
        vchain, top_red, aug_hi, aug_lo, mean_ps, mean_sb = sem("vchain"), sem("top_red"), sem("aug_hi"), sem("aug_lo"), sem("mean_ps"), sem("mean_sb")
        v_arg, v_exp, v_scaled, w_hi, w_lo = sem("v_arg"), sem("v_exp"), sem("v_scaled"), [sem(f"w_hi{m}") for m in range(2)], sem("w_lo")
        s1_spread, s1_ps, s1_set, u_arg, u_exp, u_set = sem("s1_spread"), sem("s1_ps"), sem("s1_set"), sem("u_arg"), sem("u_exp"), sem("u_set")
        edge_done, sign_done, code_done, turn_done, mask_done = sem("edge_done"), sem("sign_done"), sem("code_done"), sem("turn_done"), sem("mask_done")
        acc_done, scaled_done, both_done, num_done, y_done, norm_done = (sem(n) for n in ("acc_done", "scaled_done", "both_done", "num_done", "y_done", "norm_done"))
        h_top, tail = sem("h_top"), sem("tail")

        carried = {e: sem(f"carried_{n}") for n, e in (("pool", nc.gpsimd.engine), ("pe", nc.tensor.engine), ("dve", nc.vector.engine))}
        block = ctx.enter_context(nc.Block())

        x_tiles = x.rearrange("(q b c k) d -> q c b (k d)", q=Q, b=NB, c=32)
        adj_rows = adj.rearrange("(r s i) (q n) -> q i r s n", s=SLAB, i=32, q=Q)
        s_tiles = s_lin.rearrange("w (q b c k) -> w q c b k", q=Q, b=NB, c=32)

        def quad(q):
            return slice(32 * q, 32 * q + 32)

        def at_least(eng, semaphore, value, first):
            if not first or value > 0:
                eng.wait_ge(semaphore, value)

        def carry(eng):
            eng.sem_inc(carried[eng.engine], 1)

        @block.sync
        def _(sp):
            def slab_in(pair, i, first):
                slab = pair * 4 + i
                if not first:
                    sp.wait_ge(edge_done, slab - RING + 1)
                for q in range(Q):
                    sp.dma_start(adj_ring[quad(q), i, :].rearrange("p (s n) -> p s n", s=SLAB),
                                 adj_rows[q, :, bass.ds(slab, 1), :, :].rearrange("i r s n -> i (r s) n")).then_inc(adj_in[i], 16)

            for q in range(Q):
                sp.dma_start(x_all[quad(q)].rearrange("p b k d -> p b (k d)"), x_tiles[q]).then_inc(x_in, 16)
            slab_in(0, 0, True)
            sp.wait_ge(h_sb, NB)
            slab_in(0, 1, True)
            for i in range(2):
                sp.wait_ge(w_lo, (i + 1) * KT)
                sp.wait_ge(mean_ps, i + 1)
                slab_in(0, 2 + i, True)
            with sp.Fori(1, PAIRS) as pair:
                for i in range(4):
                    slab_in(pair, i, False)

        @block.gpsimd
        def _(pool):
            nc.gpsimd.memset(ident[:], 0.0).then_inc(ident0, 1)
            nc.gpsimd.memset(ones[:], 1.0).then_inc(consts, 1)
            nc.gpsimd.memset(minus_half[:], -0.5).then_inc(consts, 1)
            pool.wait_ge(ident0, 1)
            nc.gpsimd.affine_select(out=ident[:], in_=ident[:], compare_op=ALU.not_equal, fill=1.0, base=0,
                                    pattern=[[-1, P]], channel_multiplier=1).then_inc(consts, 1)
            pool.wait_ge(vchain, 3)
            nc.gpsimd.partition_all_reduce(top_all[:, 0:3], tops[:, 0:3], P, RMAX).then_inc(top_red, 1)

            pool.wait_ge(v_scaled, 2)
            for t in range(KT):
                nc.gpsimd.tensor_scalar(w_parts[:, t, 1, 0:D], hs[:, t, :], v_col[:, 5, t:t + 1], 1.0,
                                        ALU.mult, ALU.mult).then_inc(w_hi[1], 1)
            pool.wait_ge(mean_sb, 1)

            def sums(pair, u):
                blk = pair * 2 + u

                def step(ins, n):
                    ins.then_inc(pool_step, 1)
                    pool.wait_ge(pool_step, blk * POOL_STEPS + n)
                    carry(pool)

                pool.wait_ge(both_done, blk + 1)
                step(nc.gpsimd.tensor_tensor(den[:, u, 0:1], both[:, u, D:DA], both[:, u, MV - 1:MV], ALU.add), 1)
                nc.gpsimd.tensor_scalar(den[:, u, 1:2], den[:, u, 0:1], TINY, top_all[:, 4:5], ALU.max, ALU.mult).then_inc(den_done, 1)
                step(nc.gpsimd.tensor_scalar(den[:, u, 2:3], den[:, u, 0:1], 0.0, None, ALU.is_equal), 2)
                nc.gpsimd.tensor_tensor(num[:, u, :], both[:, u, 0:D], both[:, u, DA:MV - 1], ALU.add).then_inc(num_done, 1)
                step(nc.gpsimd.tensor_scalar(rest[:, u, :], h_mean[:], den[:, u, 2:3], 1.0, ALU.mult, ALU.mult), 3)
                pool.wait_ge(x_blk_in[u], (pair + 1) * 16)
                nc.gpsimd.tensor_tensor(rest[:, u, :], rest[:, u, :], x_blk[:, u, :], ALU.add).then_inc(rest_done, 1)

            def norm(pair, u):
                blk = pair * 2 + u

                def step(ins, n):
                    ins.then_inc(pool_step, 1)
                    pool.wait_ge(pool_step, blk * POOL_STEPS + n)
                    carry(pool)

                pool.wait_ge(y_done, blk + 2)
                carry(pool)
                step(nc.gpsimd.tensor_scalar(mv[:, u, 2:3], mv[:, u, 1:2], EPS, 1.0, ALU.add, ALU.mult), 4)
                step(nc.gpsimd.tensor_tensor(mv[:, u, 3:4], mv[:, u, 2:3], minus_half[:], ALU.pow), 5)
                nc.gpsimd.tensor_scalar(o_blk[:, u, :], y_blk[:, u, :], mv[:, u, 0:1], mv[:, u, 3:4],
                                        ALU.subtract, ALU.mult).then_inc(norm_done, 1)

            def store(pair, u):
                blk = pair * 2 + u
                pool.wait_ge(norm_done, blk + 1)
                pool.dma_start(out[bass.ds(blk * P, P), :], o_blk[:, u, :]).then_inc(out_done[u], 16)

            def both_blocks(pair, first):
                for u in range(2):
                    sums(pair, u)
                    if not first:
                        pool.wait_ge(out_done[u], pair * 16)
                    norm(pair, u)
                    store(pair, u)

            both_blocks(0, True)
            with pool.Fori(1, PAIRS) as pair:
                both_blocks(pair, False)
            for u in range(2):
                pool.wait_ge(out_done[u], PAIRS * 16)

        @block.scalar
        def _(act):
            act.dma_start(w_sb[:], w_in).then_inc(wts_in, 16)
            act.dma_start(a_col[:], a_vec.rearrange("(c o) -> o c", c=2), allow_slow_non_contiguous=True).then_inc(wts_in, 16)
            act.dma_start(bw_col[:], b_w.rearrange("(o c) -> o c", c=1), allow_slow_non_contiguous=True).then_inc(wts_in, 16)
            act.dma_start(bias_row[0:1, 0:D], b_w.rearrange("(c o) -> c o", c=1)).then_inc(wts_in, 16)
            act.dma_start(ba_sb[:], b_a.rearrange("(c o) -> c o", c=1)).then_inc(wts_in, 16)
            for g in range(NB):
                act.wait_ge(xt_ps, g + 1)
                if g >= 2:
                    act.wait_ge(h_ps, g - 1)
                nc.scalar.copy(xt[:, g % 2, :], ps_xt(g)).then_inc(xt_sb, 1)
            act.wait_ge(s_sb, NB)
            for w in range(2):
                for q in range(Q):
                    act.dma_start(s_tiles[w, q], s_col[quad(q), w, :].rearrange("p (b k) -> p b k", k=4)).then_inc(s_out, 16)
            act.wait_ge(s_out, 2 * Q * 16)
            for q in range(Q):
                act.dma_start(s2_row[quad(q), :], s_lin[1:2, q * QC:(q + 1) * QC].to_broadcast([32, QC])).then_inc(s2_row_in, 16)
            act.dma_start(s1_lin[:], s_lin[0].rearrange("(h s i) -> s h i", h=2, i=32)).then_inc(s1_lin_in, 16)
            act.dma_start(s1_blk[:], s_lin[0].rearrange("(n p) -> n p", p=P)).then_inc(s1_lin_in, 16)
            act.wait_ge(v_arg, 1)
            nc.scalar.activation(v_col[:, 2, :], v_col[:, 0, :], ACT.Exp).then_inc(v_exp, 1)
            nc.scalar.activation(v_col[:, 3, :], v_col[:, 0, :], ACT.Exp, scale=SLOPE).then_inc(v_exp, 1)
            def high(tiles):
                for t in tiles:
                    nc.scalar.mul(w_parts[:, t, 0, 0:D], hs[:, t, :], v_col[:, 4, t:t + 1]).then_inc(w_hi[0], 1)

            act.wait_ge(v_scaled, 2)
            high(range(0, HEAD))
            act.wait_ge(s2_row_in, Q * 16)
            act.wait_ge(s1_set, 1)

            def signs(blk, u, sl, first):
                slab = blk * SLABS + sl
                at_least(act, code_done, slab - 1, first)
                for s in range(SLAB):
                    col = slab * SLAB + s
                    nc.scalar.activation(sign[:, sl, s * QC:(s + 1) * QC], s2_row[:], ACT.Sign,
                                         bias=s1_stripe[:, bass.ds(col, 1)]).then_inc(sign_done, 1)

            def rows_of_block():
                act.wait_ge(mean_ps, 2)
                nc.scalar.mul(h_mean[:], ps_mean, 1.0 / N).then_inc(mean_sb, 1)
                act.wait_ge(u_arg, 1)
                nc.scalar.activation(u_row[:, 4:6, :], u_row[:, 2:4, :], ACT.Exp).then_inc(u_exp, 1)

            def scale(blk, u):
                act.wait_ge(acc_done, blk + 1)
                nc.scalar.mul(scaled[:, u, :], acc(u, 0), u_row[:, 4, bass.ds(blk, 1)]).then_inc(scaled_done, 1)

            def load_x(blk, u, first):
                if not first:
                    act.wait_ge(y_done, blk)
                act.dma_start(x_blk[:, u, :], x[bass.ds(blk * P, P), :]).then_inc(x_blk_in[u], 16)

            def iteration(pair):
                for u in range(2):
                    blk = pair * 2 + u
                    signs(blk, u, 0, False)
                    signs(blk, u, 1, False)
                    scale(blk - 2, u)
                    load_x(blk - 1, 1 - u, False)

            for u in range(2):
                signs(u, u, 0, True)
                signs(u, u, 1, True)
                if u == 0:
                    high(range(HEAD, KT))
                    rows_of_block()
                else:
                    load_x(0, 0, True)
            with act.Fori(1, PAIRS) as pair:
                iteration(pair)
            load_x(BLOCKS - 1, 1, False)
            for u in range(2):
                scale(BLOCKS - 2 + u, u)

        @block.tensor
        def _(pe):
            pe.wait_ge(consts, 3)
            pe.wait_ge(wts_in, 5 * 16)
            nc.tensor.transpose(ps_small[:, 0:D], w_sb[:], ident[:]).then_inc(wt_ps, 1)
            nc.tensor.matmul(ps_mean[:, 0:2], w_sb[:], a_col[:], start=True, stop=True).then_inc(wt_ps, 1)
            nc.tensor.matmul(ps_mean[0:1, 64:66], bw_col[:], a_col[:], start=True, stop=True).then_inc(wt_ps, 1)
            pe.wait_ge(bias_sb, 1)
            pe.wait_ge(wt_sb, 3)
            nc.tensor.matmul(ps_small[:, 256:256 + DS], ones[0:1, :], bias_row[:], start=True, stop=True).then_inc(bias_ps, 1)
            pe.wait_ge(x_in, Q * 16)

            def turn_x(g):
                if g >= 2:
                    pe.wait_ge(xt_sb, g - 1)
                for k in range(4):
                    last = nc.tensor.transpose(ps_xt(g)[:, k * P:(k + 1) * P], x_all[:, g, k, :], ident[:])
                last.then_inc(xt_ps, 1)

            turn_x(0)
            for g in range(NB):
                if g + 1 < NB:
                    turn_x(g + 1)
                pe.wait_ge(xt_sb, g + 1)
                if g >= 2:
                    pe.wait_ge(h_sb, g - 1)
                for k in range(4):
                    last = nc.tensor.matmul(ps_h(g)[:, k, 0:DS], xt[:, g % 2, k * P:(k + 1) * P], wt[:], start=True, stop=True)
                last.then_inc(h_ps, 1)
            pe.wait_ge(h_sb, NB)
            for t in range(KT):
                last = nc.tensor.matmul(ps_mean, ones[:], hs[:, t, :], start=(t == 0), stop=(t == KT - 1))
                if t % (KT // 2) == KT // 2 - 1:
                    last.then_inc(mean_ps, 1)
            pe.wait_ge(s1_spread, 1)
            for half in range(2):
                last = nc.tensor.transpose(ps_small[:, half * P:(half + 1) * P],
                                           s1_rep[:, half].rearrange("s q i -> s (q i)"), ident[:])
            nc.tensor.transpose(ps_small[:, 2 * P:2 * P + BLOCKS], s1_blk[:], ident[0:BLOCKS, 0:BLOCKS]).then_inc(s1_ps, 1)
            def block_sums(pair, u, first):
                blk = pair * 2 + u
                if not first:
                    pe.wait_ge(both_done, blk - 1)
                pe.wait_ge(mask_done, 2 * SLABS * (blk + 1))
                if not first:
                    carry(pe)
                for t in range(KT):
                    b, k = divmod(t, 4)
                    if first and u == 0:
                        pe.wait_ge(w_lo, 2 * t + 2)
                    for m in range(2):
                        o = b * 4 * P + k
                        last = nc.tensor.matmul(acc(u, m), masks8[:, u, m, o:o + 4 * (P - 1) + 1:4], w_parts[:, t, m, :],
                                                start=(t == 0), stop=(t == KT - 1))
                last.then_inc(acc_done, 1)

            for u in range(2):
                block_sums(0, u, True)
            with pe.Fori(1, PAIRS) as pair:
                for u in range(2):
                    block_sums(pair, u, False)

        @block.vector
        def _(dve):
            dve.wait_ge(wt_ps, 3)
            nc.vector.tensor_copy(wt[:, 0:D], ps_small[:, 0:D]).then_inc(wt_sb, 1)
            nc.vector.tensor_copy(wt[:, D:DS], ps_mean[:, 0:2]).then_inc(wt_sb, 1)
            nc.vector.tensor_scalar(bias_row[0:1, D:D + 1], ps_mean[0:1, 64:65], ba_sb[0:1, 0:1], None, ALU.add).then_inc(bias_sb, 1)
            nc.vector.tensor_copy(bias_row[0:1, D + 1:DS], ps_mean[0:1, 65:66]).then_inc(wt_sb, 1)
            dve.wait_ge(bias_ps, 1)
            nc.vector.tensor_copy(bias_all[:], ps_small[:, 256:256 + DS]).then_inc(bias_sb, 1)
            dve.wait_ge(bias_sb, 2)
            for g in range(NB):
                dve.wait_ge(h_ps, g + 1)
                nc.vector.tensor_tensor(s_col[:, :, 4 * g:4 * g + 4].rearrange("p w t -> p t w"), ps_h(g)[:, :, D:DS],
                                        bias_all[:, D:DS].rearrange("p (a d) -> p a d", a=1).to_broadcast([P, 4, 2]), ALU.add).then_inc(s_sb, 1)
                nc.vector.tensor_tensor(hs[:, 4 * g:4 * g + 4, :], ps_h(g)[:, :, 0:D],
                                        bias_all[:, 0:D].rearrange("p (a d) -> p a d", a=1).to_broadcast([P, 4, D]), ALU.add).then_inc(h_sb, 1)
                if g >= 1:
                    dve.wait_ge(h_sb, g)
                    nc.vector.tensor_reduce(tops[:, 4 + g - 1:4 + g], hs[:, 4 * g - 4:4 * g, :], AX.XY, ALU.max,
                                            apply_absolute_value=True).then_inc(h_top, 1)
            dve.wait_ge(h_sb, NB)
            nc.vector.tensor_reduce(tops[:, 4 + NB - 1:4 + NB], hs[:, KT - 4:KT, :], AX.XY, ALU.max,
                                    apply_absolute_value=True).then_inc(h_top, 1)
            dve.wait_ge(s_sb, NB)
            nc.vector.tensor_reduce(tops[:, 0:1], s_col[:, 1, :], AX.X, ALU.max).then_inc(vchain, 1)
            nc.vector.tensor_reduce(tops[:, 1:2], s_col[:, 1, :], AX.X, ALU.min, negate=True).then_inc(vchain, 1)
            dve.wait_ge(h_top, NB)
            nc.vector.tensor_reduce(tops[:, 2:3], tops[:, 4:4 + NB], AX.X, ALU.max).then_inc(vchain, 1)
            dve.wait_ge(top_red, 1)
            nc.vector.tensor_scalar(v_col[:, 0, :], s_col[:, 1, :], top_all[:, 0:1], None, ALU.subtract).then_inc(v_arg, 1)
            nc.vector.tensor_scalar(top_all[:, 3:4], top_all[:, 2:3], TINY, None, ALU.max).then_inc(vchain, 1)
            dve.wait_ge(vchain, 4)
            nc.vector.reciprocal(top_all[:, 4:5], top_all[:, 3:4]).then_inc(vchain, 1)
            dve.wait_ge(vchain, 5)
            dve.wait_ge(v_exp, 2)
            for m in range(2):
                nc.vector.tensor_scalar(v_col[:, 4 + m, :], v_col[:, 2 + m, :], top_all[:, 4:5], W_TOP, ALU.mult, ALU.mult).then_inc(v_scaled, 1)
            for m in range(2):
                nc.vector.tensor_scalar(w_parts[:, :, m, D], v_col[:, 2 + m, :], W_TOP, None, ALU.mult).then_inc(aug_hi, 1)
            dve.wait_ge(aug_hi, 2)
            for m in range(2):
                nc.vector.scalar_tensor_tensor(w_parts[:, :, m, MV - 1], v_col[:, 2 + m, :], W_TOP, w_parts[:, :, m, D],
                                               ALU.mult, ALU.subtract).then_inc(aug_lo, 1)
            dve.wait_ge(s1_lin_in, 32)
            nc.vector.tensor_copy(s1_rep[:], s1_lin[:].rearrange("p h (a i) -> p h a i", a=1).to_broadcast([P, 2, Q, 32])).then_inc(s1_spread, 1)
            dve.wait_ge(v_scaled, 2)

            def low(tiles):
                for t in tiles:
                    for m in range(2):
                        dve.wait_ge(w_hi[m], t + 1)
                        nc.vector.scalar_tensor_tensor(w_parts[:, t, m, DA:MV - 1], hs[:, t, :], v_col[:, 4 + m, t:t + 1],
                                                       w_parts[:, t, m, 0:D], ALU.mult, ALU.subtract).then_inc(w_lo, 1)

            def row_factors():
                nc.vector.tensor_scalar(u_row[:, 0, :], ps_small[:, 2 * P:2 * P + BLOCKS], top_all[:, 0:1], None, ALU.add).then_inc(vchain, 1)
                dve.wait_ge(vchain, 6)
                nc.vector.scalar_tensor_tensor(u_row[:, 1, :], u_row[:, 0, :], SLOPE, u_row[:, 0, :], ALU.mult, ALU.max).then_inc(vchain, 1)
                dve.wait_ge(vchain, 7)
                nc.vector.tensor_tensor(u_row[:, 2, :], u_row[:, 0, :], u_row[:, 1, :], ALU.subtract).then_inc(vchain, 1)
                nc.vector.scalar_tensor_tensor(u_row[:, 3, :], u_row[:, 0, :], SLOPE, u_row[:, 1, :], ALU.mult, ALU.subtract).then_inc(vchain, 1)
                dve.wait_ge(vchain, 9)
                nc.vector.engine_nop().then_inc(u_arg, 1)

            def edges(pair, u, sl):
                slot = u * SLABS + sl
                dve.wait_ge(adj_in[slot], (pair + 1) * Q * 16)
                nc.vector.tensor_scalar(edge[:, sl, :], adj_ring[:, slot, :], 0.0, float(EDGE), ALU.is_gt, ALU.mult).then_inc(edge_done, 1)

            def codes(pair, u, sl):
                slab = (pair * 2 + u) * SLABS + sl
                dve.wait_ge(sign_done, SLAB * (slab + 1))
                dve.wait_ge(edge_done, slab + 1)
                nc.vector.scalar_tensor_tensor(edge32[:, sl, :], sign32[:, sl, :], POS * WORD, edge32[:, sl, :],
                                               ALU.bitwise_xor, ALU.bitwise_and).then_inc(code_done, 1)

            def turns(pair, u, sl):
                slab = (pair * 2 + u) * SLABS + sl
                dve.wait_ge(code_done, slab + 1)
                nc.vector.transpose(turned[:, sl, :], edge32[:, sl, :]).then_inc(turn_done, 1)

            def split(pair, u, sl, m):
                slab = (pair * 2 + u) * SLABS + sl
                if m == 0:
                    dve.wait_ge(turn_done, slab + 1)
                src = turned[:, sl, :].rearrange("p (s b i) -> p b s i", s=SLAB, b=NB)
                nc.vector.tensor_scalar(masks[:, u, m, :, sl * SLAB:(sl + 1) * SLAB, :], src, (POS, NEG)[m] * WORD, None,
                                        ALU.bitwise_and).then_inc(mask_done, 1)

            def combine(blk, u):
                dve.wait_ge(scaled_done, blk + 1)
                nc.vector.scalar_tensor_tensor(both[:, u, :], acc(u, 1), u_row[:, 6, bass.ds(blk, 1)], scaled[:, u, :],
                                               ALU.mult, ALU.add).then_inc(both_done, 1)

            def over_den(blk, u):
                dve.wait_ge(den_done, blk + 1)
                nc.vector.reciprocal(den[:, u, 3:4], den[:, u, 1:2]).then_inc(rden_done, 1)

            def add_up(blk, u):
                dve.wait_ge(num_done, blk + 1)
                dve.wait_ge(rest_done, blk + 1)
                dve.wait_ge(rden_done, blk + 1)
                nc.vector.scalar_tensor_tensor(y_blk[:, u, :], num[:, u, :], den[:, u, 3:4], rest[:, u, :], ALU.mult, ALU.add).then_inc(tail, 1)

            def moments(blk, u):
                dve.wait_ge(tail, blk * TAIL_STEPS + 1)
                nc.vector.bn_stats(stats[:, u, :], y_blk[:, u, :]).then_inc(tail, 1)
                dve.wait_ge(tail, blk * TAIL_STEPS + 2)
                carry(dve)
                nc.vector.bn_aggr(mv[:, u, 0:2], stats[:, u, :]).then_inc(y_done, 1)

            def block_codes(pair, u):
                for stage in (edges, codes, turns):
                    for sl in range(SLABS):
                        stage(pair, u, sl)

            dve.wait_ge(s1_ps, 1)
            nc.vector.tensor_copy(s1_stripe[:], ps_small[:, 0:2 * P]).then_inc(s1_set, 1)
            row_factors()
            low(range(0, HEAD))
            block_codes(0, 0)
            for sl in range(SLABS):
                for m in range(2):
                    split(0, 0, sl, m)
            low(range(HEAD, KT))
            dve.wait_ge(u_exp, 1)
            nc.vector.tensor_scalar(u_row[:, 6, :], u_row[:, 5, :], NEG_SCALE, None, ALU.mult).then_inc(u_set, 1)
            nc.vector.engine_nop().then_inc(y_done, 1)
            dve.wait_ge(u_set, 1)
            dve.wait_ge(mean_sb, 1)
            block_codes(0, 1)
            for sl in range(SLABS):
                for m in range(2):
                    split(0, 1, sl, m)
            with dve.Fori(1, PAIRS) as pair:
                for u in range(2):
                    before = pair * 2 + u - 2
                    block_codes(pair, u)
                    combine(before, u)
                    split(pair, u, 0, 0)
                    split(pair, u, 0, 1)
                    split(pair, u, 1, 0)
                    over_den(before, u)
                    split(pair, u, 1, 1)
                    add_up(before, u)
                    moments(before, u)
            for u in range(2):
                before = BLOCKS - 2 + u
                combine(before, u)
                over_den(before, u)
                add_up(before, u)
                moments(before, u)


_INS = ["x", "adj", "L0_gnn_W", "L0_gnn_b_W", "L0_gnn_a_vec", "L0_gnn_b_a"]


def kernel(**inputs):
    import numpy as _np
    import concourse.bacc as _bacc
    from concourse import mybir as _mybir
    from concourse.bass_utils import run_bass_kernel_spmd as _run

    nc = _bacc.Bacc("TRN2", target_bir_lowering=False, num_devices=1)
    arrays, args = {}, []
    for name in _INS:
        a = _np.ascontiguousarray(inputs[name])
        arrays[f"in_{name}"] = a
        args.append(nc.dram_tensor(f"in_{name}", a.shape, _mybir.dt.from_np(a.dtype), kind="ExternalInput").ap())
    n, d = inputs["x"].shape
    out = nc.dram_tensor("out_0", (n, d), _mybir.dt.float32, kind="ExternalOutput").ap()
    s_lin = nc.dram_tensor("s_lin", (2, n), _mybir.dt.float32, kind="Internal").ap()
    gat_kernel(nc, *args, out, s_lin)
    r = _run(nc, [arrays], core_ids=[0])
    return r.results[0]["out_0"]
```

```python
import concourse.bass as bass
from concourse import mybir
from concourse.alu_op_type import AluOpType as ALU
from contextlib import ExitStack


P = 128
F32, F16, U8, U32, I8 = (mybir.dt.float32, mybir.dt.float16, mybir.dt.uint8, mybir.dt.uint32, mybir.dt.int8)
I32, F8 = mybir.dt.int32, mybir.dt.float8e4
ACT = mybir.ActivationFunctionType
AX = mybir.AxisListType
RMAX = bass.bass_isa.ReduceOp.max

D = 128
Q = 4
SP_QUADS, ACT_QUADS = (0, 1), (2, 3)
SLOPE = 0.2
X_LOADS = 4
GROUP = 8
HEAD = 3
TAIL = 1
POOL_SPLITS = 2
ACT_CASTS = (4, 6, 7)
EPS = 1e-5
EDGE = 0x78
POS, NEG = 0x38, 0x40
NEG_SCALE = 0.5
WORD = 0x01010101
W_TOP = 2.0 ** 15
TINY = 1e-30
SPREAD_MAX = 10.0
NO_EDGE = -9e15 / 0.2
FAR_STEPS = 12
POOL_STEPS = 4
TAIL_STEPS = 2


def gat_kernel(nc, x, adj, w_in, b_w, a_vec, b_a, out, s_lin):
    N = x.shape[0]
    QC = N // Q
    NB = QC // P
    KT = NB * 4
    BLOCKS = N // P
    PAIRS = BLOCKS // 2
    SLAB = 2
    SLABS = 2
    SC = SLAB * QC
    SW = SC // 4
    RING = 4
    DA = D + 1
    DS = D + 2
    MV = 2 * DA

    ctx = ExitStack()
    with ctx:
        def sb(name, shape, dt):
            return ctx.enter_context(nc.sbuf_tensor(name, shape, dt))

        def sem(name):
            return ctx.enter_context(nc.semaphore(name))

        adj_ring = sb("adj_ring", [P, RING, SC], I32)
        mask_words = sb("mask_words", [P, KT * P], U32)
        turned = sb("turned", [P, 2, SW], U32)
        w_parts = sb("w_parts", [P, KT, 2, MV], F16)
        s2_row = sb("s2_row", [P, QC], F32)
        edge = sb("edge", [P, 2, SC], U8)
        sign = sb("sign", [P, 2, SC], I8)
        scaled = sb("scaled", [P, 2, MV], F32)
        both = sb("both", [P, 2, MV], F32)
        num = sb("num", [P, 2, D], F32)
        x_blk = sb("x_blk", [P, 2, D], F32)
        y_blk = sb("y_blk", [P, 2, D], F32)
        o_blk = sb("o_blk", [P, 2, D], F32)
        h_mean = sb("h_mean", [P, D], F32)
        den = sb("den", [P, 2, 4], F32)
        rest = sb("rest", [P, 2, D], F32)
        minus_half = sb("minus_half", [P, 1], F32)
        stats = sb("stats", [P, 2, 6], F32)
        mv = sb("mv", [P, 2, 4], F32)
        row_top = sb("row_top", [P, 6 + Q], F32)
        far_flag = sb("far_flag", [P, 1], I32)
        s1_stripe = sb("s1_stripe", [P, N // 32], F32)
        u_row = sb("u_row", [P, 8, BLOCKS], F32)
        a_col = sb("a_col", [P, 2], F32)
        bw_col = sb("bw_col", [P, 1], F32)
        ba_sb = sb("ba_sb", [1, 1], F32)
        ones = sb("ones", [P, P], F32)
        v_col = sb("v_col", [P, 6, KT], F32)
        tops = sb("tops", [P, 20], F32)
        top_all = sb("top_all", [P, 8], F32)
        
        psum = ctx.enter_context(nc.psum_tensor("psum", [P, 8, 512], F32))

        early = sign[:, :, :].bitcast(F32).rearrange("p u n -> p (u n)")
        sizes = [0, D, DS, DS, DS, 2 * KT, N // P, N // 32, P, P]
        starts = [sum(sizes[:n + 1]) for n in range(len(sizes))]
        w_sb, wt, bias_row, bias_all, s_col, s1_lin, s1_rep, s1_blk, ident = (early[:, a:b] for a, b in zip(starts, starts[1:]))
        bias_row, s1_blk = bias_row[0:1], s1_blk[0:BLOCKS]
        s_col = s_col.rearrange("p (w t) -> p w t", w=2)
        s1_lin = s1_lin.rearrange("p (h i) -> p h i", h=2)
        s1_rep = s1_rep.rearrange("p (h q i) -> p h q i", h=2, q=Q)
        masks = mask_words[:, :].rearrange("p (u m b s i) -> p u m b s i", u=2, m=2, b=NB, s=4)
        masks8 = mask_words[:, :].bitcast(F8).rearrange("p (u m n) -> p u m n", u=2, m=2)
        x_all = adj_ring[:, 2:4, :].bitcast(F32).rearrange("p u n -> p (u n)").rearrange("p (b k d) -> p b k d", b=NB, k=4)
        wide = mask_words[:, KT * P // 2:].bitcast(F32).rearrange("p (m u t d) -> p m u t d", m=2, u=2, d=D)
        hs = x_all.rearrange("p b k d -> p (b k) d")
        xt = adj_ring[:, 1, :].bitcast(F32).rearrange("p (u n) -> p u n", u=SC // 512)
        edge32 = edge[:, :, :].bitcast(U32)
        sign32 = sign[:, :, :].bitcast(U32)
        acc = lambda u, m: psum[:, 2 * u + m, 0:MV]
        ps_xt = lambda g: psum[:, g % 2, :]
        ps_h = lambda g: psum[:, 2 + 2 * (g % 2):4 + 2 * (g % 2), :].rearrange("p a (b n) -> p (a b) n", b=2)
        ps_small = psum[:, 6, :]
        ps_mean = psum[:, 7, 0:D]

        adj_in = [sem(f"adj_in{r}") for r in range(RING)]
        x_in, wts_in, x_blk_in, out_done = [sem(f"x_in{c}") for c in range(X_LOADS)], sem("wts_in"), [sem(f"x_blk_in{u}") for u in range(2)], [sem(f"out_done{u}") for u in range(2)]
        s_out, s2_row_in, s1_lin_in = sem("s_out"), sem("s2_row_in"), sem("s1_lin_in")
        consts, ident0 = sem("consts"), sem("ident0")
        pool_step, den_done, rest_done, rden_done = sem("pool_step"), sem("den_done"), sem("rest_done"), sem("rden_done")
        wt_ps, wt_sb, bias_ps, bias_sb = sem("wt_ps"), sem("wt_sb"), sem("bias_ps"), sem("bias_sb")
        xt_ps, xt_sb, h_ps, h_sb, s_sb = sem("xt_ps"), sem("xt_sb"), sem("h_ps"), sem("h_sb"), sem("s_sb")
        vchain, top_red, aug_hi, aug_lo, mean_ps, mean_sb = sem("vchain"), sem("top_red"), sem("aug_hi"), sem("aug_lo"), sem("mean_ps"), sem("mean_sb")
        v_arg, v_exp, v_scaled, wide_done, w_hi, w_lo = sem("v_arg"), sem("v_exp"), sem("v_scaled"), [sem(f"wide_done{m}") for m in range(3)], [sem(f"w_hi{m}") for m in range(2)], [sem(f"w_lo{m}") for m in range(2)]
        s1_spread, s1_ps, s1_set, u_arg, u_exp, u_set = sem("s1_spread"), sem("s1_ps"), sem("s1_set"), sem("u_arg"), sem("u_exp"), sem("u_set")
        edge_done, sign_done, code_done, turn_done, mask_done = sem("edge_done"), sem("sign_done"), sem("code_done"), sem("turn_done"), sem("mask_done")
        acc_done, scaled_done, both_done, num_done, y_done, norm_done = (sem(n) for n in ("acc_done", "scaled_done", "both_done", "num_done", "y_done", "norm_done"))
        h_top, tail, end_step, std_done, eps_added, last_stored = (sem(n) for n in ("h_top", "tail", "end_step", "std_done", "eps_added", "last_stored"))

        flag_step, s2_all_in, far_in, far_norm, far_stored, far_y, far_std, far_scores, far_exp = (
            sem(n) for n in ("flag_step", "s2_all_in", "far_in", "far_norm", "far_stored", "far_y", "far_std", "far_scores", "far_exp"))
        far_turned, far_copied, far_sums, far_step = (sem(n) for n in ("far_turned", "far_copied", "far_sums", "far_step"))
        carried = {e: sem(f"carried_{n}") for n, e in (("pool", nc.gpsimd.engine), ("pe", nc.tensor.engine), ("dve", nc.vector.engine), ("sp", nc.sync.engine))}
        block = ctx.enter_context(nc.Block())

        x_tiles = x.rearrange("(q b c k) d -> q c b (k d)", q=Q, b=NB, c=32)
        adj_rows = adj.rearrange("(r s i) (q n) -> q i r s n", s=SLAB, i=32, q=Q)
        s_tiles = s_lin.rearrange("w (q b c k) -> w q c b k", q=Q, b=NB, c=32)

        def quad(q):
            return slice(32 * q, 32 * q + 32)

        groups = KT // GROUP

        adj_all = adj_ring[:, 0:2, :].rearrange("p u n -> p (u n)")
        weights = adj_all.bitcast(F32).rearrange("p (b k j) -> p b k j", b=NB, k=4)
        scores = mask_words[:, :].bitcast(F32)
        s2_all = w_parts[:, :, :, :].rearrange("p t m n -> p (t m n)")[:, 0:2 * N].bitcast(F32)
        far_turn = edge[:, :, :].bitcast(F32).rearrange("p u n -> p (u n)")[:, 0:1024].rearrange("p (u n) -> p u n", u=2)

        def far_spread(eng):
            eng.wait_ge(flag_step, 2)
            return eng.value_load(far_flag[0:1, 0:1], min_val=0, max_val=1) > 0

        def part(g, m, lo):
            return w_parts[:, g * GROUP:(g + 1) * GROUP, m, lo * DA:lo * DA + D]

        def at_least(eng, semaphore, value, first):
            if not first or value > 0:
                eng.wait_ge(semaphore, value)

        def carry(eng):
            eng.sem_inc(carried[eng.engine], 1)

        def slab_in(eng, pair, i, quads, first):
            slab = pair * 4 + i
            if not first:
                eng.wait_ge(edge_done, slab - RING + 1)
            for q in quads:
                eng.dma_start(adj_ring[quad(q), i, :].rearrange("p (s n) -> p s n", s=SLAB),
                              adj_rows[q, :, bass.ds(slab, 1), :, :].rearrange("i r s n -> i (r s) n")).then_inc(adj_in[i], 16)

        @block.sync
        def _(sp):
            def stripe_in(i, s):
                for q in (0, 2, 1, 3):
                    sp.dma_start(adj_ring[quad(q), i, s * QC:(s + 1) * QC], adj_rows[q, :, i, s, :]).then_inc(adj_in[i], 16)

            for c in range(X_LOADS):
                piece = slice(c * NB // X_LOADS, (c + 1) * NB // X_LOADS)
                for q in range(Q):
                    sp.dma_start(x_all[quad(q), piece].rearrange("p b k d -> p b (k d)"), x_tiles[q, :, piece]).then_inc(x_in[c], 16)
            slab_in(sp, 0, 0, SP_QUADS, True)
            sp.wait_ge(h_sb, NB)
            sp.wait_ge(s_sb, NB)
            for w in range(2):
                for q in range(Q):
                    sp.dma_start(s_tiles[w, q], s_col[quad(q), w, :].rearrange("p (b k) -> p b k", k=4)).then_inc(s_out, 16)
            sp.wait_ge(s_out, 2 * Q * 16)
            for q in range(Q):
                sp.dma_start(s2_row[quad(q), :], s_lin[1:2, q * QC:(q + 1) * QC].to_broadcast([32, QC])).then_inc(s2_row_in, 16)
            sp.dma_start(s1_lin[:], s_lin[0].rearrange("(h s i) -> s h i", h=2, i=32)).then_inc(s1_lin_in, 16)
            sp.dma_start(s1_blk[:], s_lin[0].rearrange("(n p) -> n p", p=P)).then_inc(s1_lin_in, 16)
            slab_in(sp, 0, 1, SP_QUADS, True)
            with sp.If(far_spread(sp)):
                for i in range(SLABS):
                    sp.wait_ge(adj_in[i], Q * 16)
                sp.dma_start(s2_all, s_lin[1:2, :].to_broadcast([P, N])).then_inc(s2_all_in, 16)
                with sp.Fori(0, BLOCKS) as blk:
                    sp.dma_start(adj_all, adj[bass.ds(blk * P, P), :]).then_inc(far_in, 16)
                    sp.dma_start(x_blk[:, 0, :], x[bass.ds(blk * P, P), :]).then_inc(far_in, 16)
                    sp.wait_ge(far_norm, blk + 1)
                    sp.dma_start(out[bass.ds(blk * P, P), :], o_blk[:, 0, :]).then_inc(far_stored, 16)
                    sp.wait_ge(far_stored, (blk + 1) * 16)
                    carry(sp)

            with sp.Else():
                for i in range(2):
                    sp.wait_ge(mean_ps, i + 1)
                    for s in range(SLAB):
                        until = (SLAB * i + s + 1) * groups // (2 * SLAB)
                        sp.wait_ge(wide_done[0], min(until, groups - TAIL))
                        sp.wait_ge(wide_done[1], until)
                        if until > groups - TAIL:
                            sp.wait_ge(wide_done[2], until - (groups - TAIL))
                        stripe_in(2 + i, s)
                with sp.Fori(1, PAIRS) as pair:
                    for i in range(4):
                        slab_in(sp, pair, i, SP_QUADS, False)
                sp.wait_ge(norm_done, BLOCKS)
                sp.dma_start(out[(BLOCKS - 1) * P:, :], o_blk[:, 1, :]).then_inc(last_stored, 16)
                sp.wait_ge(last_stored, 16)

        @block.gpsimd
        def _(pool):
            nc.gpsimd.memset(ident[:], 0.0).then_inc(ident0, 1)
            nc.gpsimd.memset(ones[:], 1.0).then_inc(consts, 1)
            nc.gpsimd.memset(minus_half[:], -0.5).then_inc(consts, 1)
            pool.wait_ge(ident0, 1)
            nc.gpsimd.affine_select(out=ident[:], in_=ident[:], compare_op=ALU.not_equal, fill=1.0, base=0,
                                    pattern=[[-1, P]], channel_multiplier=1).then_inc(consts, 1)
            pool.wait_ge(vchain, 3)
            nc.gpsimd.partition_all_reduce(top_all[:, 0:3], tops[:, 0:3], P, RMAX).then_inc(top_red, 1)

            with pool.If(far_spread(pool)):
                with pool.Fori(0, BLOCKS) as blk:
                    pool.wait_ge(far_y, blk + 1)
                    carry(pool)
                    nc.gpsimd.tensor_scalar(mv[:, 0, 2:3], mv[:, 0, 1:2], EPS, 1.0, ALU.add, ALU.mult).then_inc(far_std, 1)
                    pool.wait_ge(far_std, 2 * blk + 1)
                    carry(pool)
                    nc.gpsimd.tensor_tensor(mv[:, 0, 3:4], mv[:, 0, 2:3], minus_half[:], ALU.pow).then_inc(far_std, 1)
                    pool.wait_ge(far_std, 2 * blk + 2)
                    carry(pool)
                    nc.gpsimd.tensor_scalar(o_blk[:, 0, :], y_blk[:, 0, :], mv[:, 0, 0:1], mv[:, 0, 3:4],
                                            ALU.subtract, ALU.mult).then_inc(far_norm, 1)
            with pool.Else():
                pool.wait_ge(v_scaled, 2)
                for m, some in ((1, range(groups)), (0, range(groups - TAIL, groups))):
                    for g in some:
                        if g >= 2:
                            pool.wait_ge(w_lo[m], g - 1)
                        for t in range(GROUP):
                            last = nc.gpsimd.tensor_scalar(wide[:, m, g % 2, t, :], hs[:, g * GROUP + t, :],
                                                           v_col[:, 4 + m, g * GROUP + t:g * GROUP + t + 1], 1.0, ALU.mult, ALU.mult)
                        last.then_inc(wide_done[m or 2], 1)
                        if m == 1 and g == POOL_SPLITS:
                            pool.wait_ge(w_hi[1], g)
                            pool.wait_ge(wide_done[1], g + 1)
                            nc.gpsimd.tensor_copy(part(g, 1, 0), wide[:, 1, g % 2]).then_inc(w_hi[1], 1)
                            pool.wait_ge(w_hi[1], g + 1)
                            pool.wait_ge(w_lo[1], g)
                            nc.gpsimd.tensor_tensor(part(g, 1, 1), wide[:, 1, g % 2], part(g, 1, 0), ALU.subtract).then_inc(w_lo[1], 1)
                pool.wait_ge(mean_sb, 1)

                def sums(pair, u):
                    blk = pair * 2 + u

                    def step(ins, n):
                        ins.then_inc(pool_step, 1)
                        pool.wait_ge(pool_step, blk * POOL_STEPS + n)
                        carry(pool)

                    pool.wait_ge(both_done, blk + 1)
                    step(nc.gpsimd.tensor_tensor(den[:, u, 0:1], both[:, u, D:DA], both[:, u, MV - 1:MV], ALU.add), 1)
                    nc.gpsimd.tensor_scalar(den[:, u, 1:2], den[:, u, 0:1], TINY, top_all[:, 4:5], ALU.max, ALU.mult).then_inc(den_done, 1)
                    step(nc.gpsimd.tensor_scalar(den[:, u, 2:3], den[:, u, 0:1], 0.0, None, ALU.is_equal), 2)
                    nc.gpsimd.tensor_tensor(num[:, u, :], both[:, u, 0:D], both[:, u, DA:MV - 1], ALU.add).then_inc(num_done, 1)
                    step(nc.gpsimd.tensor_scalar(rest[:, u, :], h_mean[:], den[:, u, 2:3], 1.0, ALU.mult, ALU.mult), 3)
                    pool.wait_ge(x_blk_in[u], (pair + 1) * 16)
                    nc.gpsimd.tensor_tensor(rest[:, u, :], rest[:, u, :], x_blk[:, u, :], ALU.add).then_inc(rest_done, 1)

                def inverse_std(pair, u):
                    blk = pair * 2 + u
                    pool.wait_ge(y_done, blk + 2)
                    carry(pool)
                    nc.gpsimd.tensor_scalar(mv[:, u, 2:3], mv[:, u, 1:2], EPS, 1.0, ALU.add, ALU.mult).then_inc(eps_added, 1)
                    pool.wait_ge(eps_added, blk + 1)
                    carry(pool)
                    return nc.gpsimd.tensor_tensor(mv[:, u, 3:4], mv[:, u, 2:3], minus_half[:], ALU.pow)

                def norm(pair, u):
                    blk = pair * 2 + u
                    inverse_std(pair, u).then_inc(pool_step, 1)
                    pool.wait_ge(pool_step, (blk + 1) * POOL_STEPS)
                    carry(pool)
                    nc.gpsimd.tensor_scalar(o_blk[:, u, :], y_blk[:, u, :], mv[:, u, 0:1], mv[:, u, 3:4],
                                            ALU.subtract, ALU.mult).then_inc(norm_done, 1)

                def store(pair, u):
                    blk = pair * 2 + u
                    pool.wait_ge(norm_done, blk + 1)
                    pool.dma_start(out[bass.ds(blk * P, P), :], o_blk[:, u, :]).then_inc(out_done[u], 16)

                def both_blocks(pair, first):
                    for u in range(2):
                        sums(pair, u)
                        if not first:
                            pool.wait_ge(out_done[u], pair * 16)
                        norm(pair, u)
                        store(pair, u)

                both_blocks(0, True)
                with pool.Fori(1, PAIRS - 1) as pair:
                    both_blocks(pair, False)
                sums(PAIRS - 1, 0)
                pool.wait_ge(out_done[0], (PAIRS - 1) * 16)
                norm(PAIRS - 1, 0)
                store(PAIRS - 1, 0)
                inverse_std(PAIRS - 1, 1).then_inc(std_done, 1)
                pool.wait_ge(out_done[0], PAIRS * 16)

        @block.scalar
        def _(act):
            act.dma_start(w_sb[:], w_in).then_inc(wts_in, 16)
            act.dma_start(a_col[:], a_vec.rearrange("(c o) -> o c", c=2), allow_slow_non_contiguous=True).then_inc(wts_in, 16)
            act.dma_start(bw_col[:], b_w.rearrange("(o c) -> o c", c=1), allow_slow_non_contiguous=True).then_inc(wts_in, 16)
            act.dma_start(bias_row[0:1, 0:D], b_w.rearrange("(c o) -> c o", c=1)).then_inc(wts_in, 16)
            act.dma_start(ba_sb[:], b_a.rearrange("(c o) -> c o", c=1)).then_inc(wts_in, 16)
            for g in range(NB):
                act.wait_ge(xt_ps, g + 1)
                if g >= 2:
                    act.wait_ge(h_ps, g - 1)
                nc.scalar.copy(xt[:, g % 2, :], ps_xt(g)).then_inc(xt_sb, 1)
                if g == X_LOADS:
                    slab_in(act, 0, 0, ACT_QUADS, True)
            act.wait_ge(h_sb, NB)
            slab_in(act, 0, 1, ACT_QUADS, True)
            act.wait_ge(v_arg, 1)
            nc.scalar.activation(v_col[:, 2, :], v_col[:, 0, :], ACT.Exp).then_inc(v_exp, 1)
            nc.scalar.activation(v_col[:, 3, :], v_col[:, 0, :], ACT.Exp, scale=SLOPE).then_inc(v_exp, 1)
            with act.If(far_spread(act)):
                with act.Fori(0, BLOCKS) as blk:
                    act.wait_ge(far_scores, blk + 1)
                    for q in range(Q):
                        last = nc.scalar.activation(weights[:, :, :, quad(q)].rearrange("p b k c -> p b c k"),
                                                    scores[:, q * QC:(q + 1) * QC].rearrange("p (b c k) -> p b c k", b=NB, c=32),
                                                    ACT.Exp, bias=row_top[:, 3:4], accum_out=row_top[:, 6 + q:7 + q])
                    last.then_inc(far_exp, 1)
            with act.Else():
                def high(some):
                    for g in some:
                        if g >= 2:
                            act.wait_ge(w_lo[0], g - 1)
                        for t in range(GROUP):
                            last = nc.scalar.mul(wide[:, 0, g % 2, t, :], hs[:, g * GROUP + t, :],
                                                 v_col[:, 4, g * GROUP + t:g * GROUP + t + 1])
                        last.then_inc(wide_done[0], 1)
                        act.wait_ge(wide_done[0], g + 1)
                        nc.scalar.copy(part(g, 0, 0), wide[:, 0, g % 2]).then_inc(w_hi[0], 1)

                def cast(g):
                    act.wait_ge(wide_done[1], g + 1)
                    act.wait_ge(w_hi[1], g)
                    nc.scalar.copy(part(g, 1, 0), wide[:, 1, g % 2]).then_inc(w_hi[1], 1)

                act.wait_ge(v_scaled, 2)
                high(range(0, HEAD))
                act.wait_ge(s2_row_in, Q * 16)
                act.wait_ge(s1_set, 1)

                def signs(blk, u, sl, first):
                    slab = blk * SLABS + sl
                    at_least(act, code_done, slab - 1, first)
                    for s in range(SLAB):
                        col = slab * SLAB + s
                        nc.scalar.activation(sign[:, sl, s * QC:(s + 1) * QC], s2_row[:], ACT.Sign,
                                             bias=s1_stripe[:, bass.ds(col, 1)]).then_inc(sign_done, 1)

                def rows_of_block():
                    act.wait_ge(mean_ps, 2)
                    nc.scalar.mul(h_mean[:], ps_mean, 1.0 / N).then_inc(mean_sb, 1)
                    act.wait_ge(u_arg, 1)
                    nc.scalar.activation(u_row[:, 4:6, :], u_row[:, 2:4, :], ACT.Exp).then_inc(u_exp, 1)

                def scale(blk, u):
                    act.wait_ge(acc_done, 2 * blk + 1)
                    nc.scalar.mul(scaled[:, u, :], acc(u, 0), u_row[:, 4, bass.ds(blk, 1)]).then_inc(scaled_done, 1)

                def load_x(blk, u, first):
                    if not first:
                        act.wait_ge(y_done, blk)
                    act.dma_start(x_blk[:, u, :], x[bass.ds(blk * P, P), :]).then_inc(x_blk_in[u], 16)

                def next_slabs(pair, u):
                    for sl in range(SLABS):
                        slab_in(act, pair + 1, u * SLABS + sl, ACT_QUADS, False)

                def iteration(pair, last):
                    for u in range(2):
                        blk = pair * 2 + u
                        signs(blk, u, 0, False)
                        signs(blk, u, 1, False)
                        if not last:
                            next_slabs(pair, u)
                        scale(blk - 2, u)
                        load_x(blk - 1, 1 - u, False)

                for u in range(2):
                    signs(u, u, 0, True)
                    signs(u, u, 1, True)
                    if u == 0:
                        next_slabs(0, 0)
                        high(range(HEAD, ACT_CASTS[0] + 1))
                        cast(ACT_CASTS[0])
                        high(range(ACT_CASTS[0] + 1, groups - TAIL))
                        for g in ACT_CASTS[1:]:
                            cast(g)
                        rows_of_block()
                    else:
                        load_x(0, 0, True)
                        next_slabs(0, 1)
                with act.Fori(1, PAIRS - 1) as pair:
                    iteration(pair, False)
                iteration(PAIRS - 1, True)
                load_x(BLOCKS - 1, 1, False)
                for u in range(2):
                    scale(BLOCKS - 2 + u, u)

        @block.tensor
        def _(pe):
            pe.wait_ge(consts, 3)
            pe.wait_ge(wts_in, 5 * 16)
            nc.tensor.transpose(ps_small[:, 0:D], w_sb[:], ident[:]).then_inc(wt_ps, 1)
            nc.tensor.matmul(ps_mean[:, 0:2], w_sb[:], a_col[:], start=True, stop=True).then_inc(wt_ps, 1)
            nc.tensor.matmul(ps_mean[0:1, 64:66], bw_col[:], a_col[:], start=True, stop=True).then_inc(wt_ps, 1)
            pe.wait_ge(bias_sb, 1)
            pe.wait_ge(wt_sb, 3)
            nc.tensor.matmul(ps_small[:, 256:256 + DS], ones[0:1, :], bias_row[:], start=True, stop=True).then_inc(bias_ps, 1)
            def turn_x(g):
                if g % (NB // X_LOADS) == 0:
                    pe.wait_ge(x_in[g // (NB // X_LOADS)], Q * 16)
                if g >= 2:
                    pe.wait_ge(xt_sb, g - 1)
                for k in range(4):
                    last = nc.tensor.transpose(ps_xt(g)[:, k * P:(k + 1) * P], x_all[:, g, k, :], ident[:])
                last.then_inc(xt_ps, 1)

            turn_x(0)
            for g in range(NB):
                if g + 1 < NB:
                    turn_x(g + 1)
                pe.wait_ge(xt_sb, g + 1)
                if g >= 2:
                    pe.wait_ge(h_sb, g - 1)
                for k in range(4):
                    last = nc.tensor.matmul(ps_h(g)[:, k, 0:DS], xt[:, g % 2, k * P:(k + 1) * P], wt[:], start=True, stop=True)
                last.then_inc(h_ps, 1)
            pe.wait_ge(h_sb, NB)
            def mean_half(half):
                for t in range(half * KT // 2, (half + 1) * KT // 2):
                    last = nc.tensor.matmul(ps_mean, ones[:], hs[:, t, :], start=(t == 0), stop=(t == KT - 1))
                last.then_inc(mean_ps, 1)

            mean_half(0)
            pe.wait_ge(s1_spread, 1)
            for half in range(2):
                last = nc.tensor.transpose(ps_small[:, half * P:(half + 1) * P],
                                           s1_rep[:, half].rearrange("s q i -> s (q i)"), ident[:])
            nc.tensor.transpose(ps_small[:, 2 * P:2 * P + BLOCKS], s1_blk[:], ident[0:BLOCKS, 0:BLOCKS]).then_inc(s1_ps, 1)
            mean_half(1)
            with pe.If(far_spread(pe)):
                with pe.Fori(0, BLOCKS) as blk:
                    pe.wait_ge(far_exp, blk + 1)
                    for g in range(NB):
                        if g >= 2:
                            pe.wait_ge(far_copied, blk * NB + g - 1)
                        for k in range(4):
                            last = nc.tensor.transpose(psum[:, g % 2, k * P:(k + 1) * P],
                                                       weights[:, g, k, :], ident[:])
                        last.then_inc(far_turned, 1)
                        pe.wait_ge(far_copied, blk * NB + g + 1)
                        for k in range(4):
                            last = nc.tensor.matmul(psum[:, 2, 0:D], far_turn[:, g % 2, k * P:(k + 1) * P], hs[:, 4 * g + k, :],
                                                    start=(g + k == 0), stop=(g == NB - 1 and k == 3))
                    last.then_inc(far_sums, 1)
            with pe.Else():
                def block_sums(pair, u, first):
                    blk = pair * 2 + u
                    if not first:
                        pe.wait_ge(both_done, blk - 1)
                    for m in range(2):
                        pe.wait_ge(mask_done, 2 * SLABS * blk + SLABS * (2 if first and u == 0 else m + 1))
                        if not first:
                            carry(pe)
                        for t in range(KT):
                            b, k = divmod(t, 4)
                            if first and u == 0 and t % GROUP == 0:
                                pe.wait_ge(w_lo[m], t // GROUP + 1)
                            o = b * 4 * P + k
                            last = nc.tensor.matmul(acc(u, m), masks8[:, u, m, o:o + 4 * (P - 1) + 1:4], w_parts[:, t, m, :],
                                                    start=(t == 0), stop=(t == KT - 1))
                        last.then_inc(acc_done, 1)

                pe.wait_ge(w_lo[0], groups - 2)
                for u in range(2):
                    block_sums(0, u, True)
                with pe.Fori(1, PAIRS) as pair:
                    for u in range(2):
                        block_sums(pair, u, False)

        @block.vector
        def _(dve):
            def edges(pair, u, sl):
                slot = u * SLABS + sl
                dve.wait_ge(adj_in[slot], pair * Q * 16 + (Q if slot < 2 else SLAB * Q) * 16)
                nc.vector.tensor_scalar(edge[:, sl, :], adj_ring[:, slot, :], 0.0, float(EDGE), ALU.is_gt, ALU.mult).then_inc(edge_done, 1)

            dve.wait_ge(wt_ps, 3)
            nc.vector.tensor_copy(wt[:, 0:D], ps_small[:, 0:D]).then_inc(wt_sb, 1)
            nc.vector.tensor_copy(wt[:, D:DS], ps_mean[:, 0:2]).then_inc(wt_sb, 1)
            nc.vector.tensor_scalar(bias_row[0:1, D:D + 1], ps_mean[0:1, 64:65], ba_sb[0:1, 0:1], None, ALU.add).then_inc(bias_sb, 1)
            nc.vector.tensor_copy(bias_row[0:1, D + 1:DS], ps_mean[0:1, 65:66]).then_inc(wt_sb, 1)
            dve.wait_ge(bias_ps, 1)
            nc.vector.tensor_copy(bias_all[:], ps_small[:, 256:256 + DS]).then_inc(bias_sb, 1)
            dve.wait_ge(bias_sb, 2)
            for g in range(NB):
                dve.wait_ge(h_ps, g + 1)
                nc.vector.tensor_tensor(s_col[:, :, 4 * g:4 * g + 4].rearrange("p w t -> p t w"), ps_h(g)[:, :, D:DS],
                                        bias_all[:, D:DS].rearrange("p (a d) -> p a d", a=1).to_broadcast([P, 4, 2]), ALU.add).then_inc(s_sb, 1)
                nc.vector.tensor_tensor(hs[:, 4 * g:4 * g + 4, :], ps_h(g)[:, :, 0:D],
                                        bias_all[:, 0:D].rearrange("p (a d) -> p a d", a=1).to_broadcast([P, 4, D]), ALU.add).then_inc(h_sb, 1)
                if g >= 1:
                    dve.wait_ge(h_sb, g)
                    nc.vector.tensor_reduce(tops[:, 4 + g - 1:4 + g], hs[:, 4 * g - 4:4 * g, :], AX.XY, ALU.max,
                                            apply_absolute_value=True).then_inc(h_top, 1)
            dve.wait_ge(h_sb, NB)
            nc.vector.tensor_reduce(tops[:, 4 + NB - 1:4 + NB], hs[:, KT - 4:KT, :], AX.XY, ALU.max,
                                    apply_absolute_value=True).then_inc(h_top, 1)
            dve.wait_ge(s_sb, NB)
            nc.vector.tensor_reduce(tops[:, 0:1], s_col[:, 1, :], AX.X, ALU.max).then_inc(vchain, 1)
            nc.vector.tensor_reduce(tops[:, 1:2], s_col[:, 1, :], AX.X, ALU.min, negate=True).then_inc(vchain, 1)
            dve.wait_ge(h_top, NB)
            nc.vector.tensor_reduce(tops[:, 2:3], tops[:, 4:4 + NB], AX.X, ALU.max).then_inc(vchain, 1)
            dve.wait_ge(top_red, 1)
            nc.vector.tensor_tensor(top_all[:, 5:6], top_all[:, 0:1], top_all[:, 1:2], ALU.add).then_inc(flag_step, 1)
            dve.wait_ge(flag_step, 1)
            nc.vector.tensor_scalar(far_flag[:], top_all[:, 5:6], SPREAD_MAX, None, ALU.is_gt).then_inc(flag_step, 1)
            nc.vector.tensor_scalar(v_col[:, 0, :], s_col[:, 1, :], top_all[:, 0:1], None, ALU.subtract).then_inc(v_arg, 1)
            nc.vector.tensor_scalar(top_all[:, 3:4], top_all[:, 2:3], TINY, None, ALU.max).then_inc(vchain, 1)
            dve.wait_ge(vchain, 4)
            nc.vector.reciprocal(top_all[:, 4:5], top_all[:, 3:4]).then_inc(vchain, 1)
            dve.wait_ge(vchain, 5)
            dve.wait_ge(v_exp, 2)
            for m in range(2):
                nc.vector.tensor_scalar(v_col[:, 4 + m, :], v_col[:, 2 + m, :], top_all[:, 4:5], W_TOP, ALU.mult, ALU.mult).then_inc(v_scaled, 1)
            with dve.If(far_spread(dve)):
                dve.wait_ge(s1_lin_in, 32)
                nc.vector.tensor_copy(s1_rep[:], s1_lin[:].rearrange("p h (a i) -> p h a i", a=1).to_broadcast([P, 2, Q, 32])).then_inc(s1_spread, 1)
                dve.wait_ge(s1_ps, 1)
                nc.vector.tensor_copy(u_row[:, 0, :], ps_small[:, 2 * P:2 * P + BLOCKS]).then_inc(s1_set, 1)
                dve.wait_ge(s1_set, 1)
                dve.wait_ge(s2_all_in, 16)
                with dve.Fori(0, BLOCKS) as blk:
                    n = [0]

                    def step(ins):
                        n[0] += 1
                        ins.then_inc(far_step, 1)
                        dve.wait_ge(far_step, blk * FAR_STEPS + n[0])

                    dve.wait_ge(far_in, (blk + 1) * 32)
                    step(nc.vector.tensor_scalar(scores, adj_all, 0.0, NO_EDGE, ALU.is_le, ALU.mult))
                    step(nc.vector.tensor_tensor(scores, scores, s2_all, ALU.add))
                    step(nc.vector.tensor_reduce(row_top[:, 0:1], scores, AX.X, ALU.max))
                    step(nc.vector.tensor_copy(row_top[:, 5:6], u_row[:, 0, bass.ds(blk, 1)]))
                    step(nc.vector.tensor_scalar(row_top[:, 1:2], row_top[:, 0:1], row_top[:, 5:6], None, ALU.add))
                    step(nc.vector.scalar_tensor_tensor(row_top[:, 2:3], row_top[:, 1:2], SLOPE, row_top[:, 1:2], ALU.mult, ALU.max))
                    step(nc.vector.tensor_scalar(row_top[:, 3:4], row_top[:, 2:3], -1.0, None, ALU.mult))
                    step(nc.vector.tensor_scalar(scores, scores, row_top[:, 5:6], None, ALU.add))
                    nc.vector.scalar_tensor_tensor(scores, scores, SLOPE, scores, ALU.mult, ALU.max).then_inc(far_scores, 1)
                    for g in range(NB):
                        dve.wait_ge(far_turned, blk * NB + g + 1)
                        nc.vector.tensor_copy(far_turn[:, g % 2, :], psum[:, g % 2, :]).then_inc(far_copied, 1)
                    dve.wait_ge(far_sums, blk + 1)
                    step(nc.vector.tensor_reduce(row_top[:, 4:5], row_top[:, 6:6 + Q], AX.X, ALU.add))
                    step(nc.vector.reciprocal(row_top[:, 5:6], row_top[:, 4:5]))
                    step(nc.vector.scalar_tensor_tensor(y_blk[:, 0, :], psum[:, 2, 0:D], row_top[:, 5:6], x_blk[:, 0, :], ALU.mult, ALU.add))
                    step(nc.vector.bn_stats(stats[:, 0, :], y_blk[:, 0, :]))
                    carry(dve)
                    nc.vector.bn_aggr(mv[:, 0, 0:2], stats[:, 0, :]).then_inc(far_y, 1)
            with dve.Else():
                for m in range(2):
                    nc.vector.tensor_scalar(w_parts[:, :, m, D], v_col[:, 2 + m, :], W_TOP, None, ALU.mult).then_inc(aug_hi, 1)
                dve.wait_ge(aug_hi, 2)
                for m in range(2):
                    nc.vector.scalar_tensor_tensor(w_parts[:, :, m, MV - 1], v_col[:, 2 + m, :], W_TOP, w_parts[:, :, m, D],
                                                   ALU.mult, ALU.subtract).then_inc(aug_lo, 1)
                dve.wait_ge(v_scaled, 2)

                def low(g, m):
                    if (m == 1 and g not in ACT_CASTS) or (m == 0 and g >= groups - TAIL):
                        if m == 1:
                            dve.wait_ge(wide_done[1], g + 1)
                        else:
                            dve.wait_ge(wide_done[2], g + 1 - (groups - TAIL))
                        nc.vector.tensor_copy(part(g, m, 0), wide[:, m, g % 2]).then_inc(w_hi[m], 1)
                    dve.wait_ge(w_hi[m], g + 1)
                    nc.vector.tensor_tensor(part(g, m, 1), wide[:, m, g % 2], part(g, m, 0), ALU.subtract).then_inc(w_lo[m], 1)

                def row_factors():
                    nc.vector.tensor_scalar(u_row[:, 0, :], ps_small[:, 2 * P:2 * P + BLOCKS], top_all[:, 0:1], None, ALU.add).then_inc(vchain, 1)
                    dve.wait_ge(vchain, 6)
                    nc.vector.scalar_tensor_tensor(u_row[:, 1, :], u_row[:, 0, :], SLOPE, u_row[:, 0, :], ALU.mult, ALU.max).then_inc(vchain, 1)
                    dve.wait_ge(vchain, 7)
                    nc.vector.tensor_tensor(u_row[:, 2, :], u_row[:, 0, :], u_row[:, 1, :], ALU.subtract).then_inc(vchain, 1)
                    nc.vector.scalar_tensor_tensor(u_row[:, 3, :], u_row[:, 0, :], SLOPE, u_row[:, 1, :], ALU.mult, ALU.subtract).then_inc(vchain, 1)
                    dve.wait_ge(vchain, 9)
                    nc.vector.engine_nop().then_inc(u_arg, 1)

                def codes(pair, u, sl):
                    slab = (pair * 2 + u) * SLABS + sl
                    dve.wait_ge(sign_done, SLAB * (slab + 1))
                    dve.wait_ge(edge_done, slab + 1)
                    nc.vector.scalar_tensor_tensor(edge32[:, sl, :], sign32[:, sl, :], POS * WORD, edge32[:, sl, :],
                                                   ALU.bitwise_xor, ALU.bitwise_and).then_inc(code_done, 1)

                def turns(pair, u, sl):
                    slab = (pair * 2 + u) * SLABS + sl
                    dve.wait_ge(code_done, slab + 1)
                    nc.vector.transpose(turned[:, sl, :], edge32[:, sl, :]).then_inc(turn_done, 1)

                def split(pair, u, sl, m):
                    slab = (pair * 2 + u) * SLABS + sl
                    if m == 0:
                        dve.wait_ge(turn_done, slab + 1)
                    src = turned[:, sl, :].rearrange("p (s b i) -> p b s i", s=SLAB, b=NB)
                    nc.vector.tensor_scalar(masks[:, u, m, :, sl * SLAB:(sl + 1) * SLAB, :], src, (POS, NEG)[m] * WORD, None,
                                            ALU.bitwise_and).then_inc(mask_done, 1)

                def combine(blk, u):
                    dve.wait_ge(acc_done, 2 * blk + 2)
                    dve.wait_ge(scaled_done, blk + 1)
                    nc.vector.scalar_tensor_tensor(both[:, u, :], acc(u, 1), u_row[:, 6, bass.ds(blk, 1)], scaled[:, u, :],
                                                   ALU.mult, ALU.add).then_inc(both_done, 1)

                def over_den(blk, u):
                    dve.wait_ge(den_done, blk + 1)
                    nc.vector.reciprocal(den[:, u, 3:4], den[:, u, 1:2]).then_inc(rden_done, 1)

                def add_up(blk, u):
                    dve.wait_ge(num_done, blk + 1)
                    dve.wait_ge(rest_done, blk + 1)
                    dve.wait_ge(rden_done, blk + 1)
                    nc.vector.scalar_tensor_tensor(y_blk[:, u, :], num[:, u, :], den[:, u, 3:4], rest[:, u, :], ALU.mult, ALU.add).then_inc(tail, 1)

                def moments(blk, u):
                    dve.wait_ge(tail, blk * TAIL_STEPS + 1)
                    nc.vector.bn_stats(stats[:, u, :], y_blk[:, u, :]).then_inc(tail, 1)
                    dve.wait_ge(tail, blk * TAIL_STEPS + 2)
                    carry(dve)
                    nc.vector.bn_aggr(mv[:, u, 0:2], stats[:, u, :]).then_inc(y_done, 1)

                def block_codes(pair, u):
                    for stage in (edges, codes, turns):
                        for sl in range(SLABS):
                            stage(pair, u, sl)

                edges(0, 0, 0)
                low(0, 0)
                low(0, 1)
                low(1, 0)
                dve.wait_ge(s1_lin_in, 32)
                nc.vector.tensor_copy(s1_rep[:], s1_lin[:].rearrange("p h (a i) -> p h a i", a=1).to_broadcast([P, 2, Q, 32])).then_inc(s1_spread, 1)
                low(1, 1)
                dve.wait_ge(s1_ps, 1)
                nc.vector.tensor_copy(s1_stripe[:], ps_small[:, 0:2 * P]).then_inc(s1_set, 1)
                row_factors()
                low(2, 0)
                edges(0, 0, 1)
                for sl in range(SLABS):
                    if sl == 1:
                        dve.wait_ge(w_lo[1], POOL_SPLITS + 1)
                        low(3, 1)
                    codes(0, 0, sl)
                    turns(0, 0, sl)
                    for m in range(2):
                        split(0, 0, sl, m)
                for g, m in ((3, 0), (4, 1), (4, 0), (5, 1), (5, 0)):
                    low(g, m)
                edges(0, 1, 0)
                for g, m in ((6, 1), (6, 0), (7, 1), (7, 0)):
                    low(g, m)
                dve.wait_ge(u_exp, 1)
                nc.vector.tensor_scalar(u_row[:, 6, :], u_row[:, 5, :], NEG_SCALE, None, ALU.mult).then_inc(u_set, 1)
                nc.vector.engine_nop().then_inc(y_done, 1)
                dve.wait_ge(u_set, 1)
                for m in range(2):
                    dve.wait_ge(w_lo[m], groups)
                dve.wait_ge(mean_sb, 1)
                for sl in range(SLABS):
                    if sl > 0:
                        edges(0, 1, sl)
                    codes(0, 1, sl)
                    turns(0, 1, sl)
                    split(0, 1, sl, 0)
                for sl in range(SLABS):
                    split(0, 1, sl, 1)
                with dve.Fori(1, PAIRS) as pair:
                    for u in range(2):
                        before = pair * 2 + u - 2
                        block_codes(pair, u)
                        combine(before, u)
                        split(pair, u, 0, 0)
                        split(pair, u, 1, 0)
                        split(pair, u, 0, 1)
                        over_den(before, u)
                        split(pair, u, 1, 1)
                        add_up(before, u)
                        moments(before, u)
                combine(BLOCKS - 2, 0)
                over_den(BLOCKS - 2, 0)
                add_up(BLOCKS - 2, 0)
                moments(BLOCKS - 2, 0)

                u, n = 1, [0]

                def then(*steps):
                    for ins in steps:
                        ins.then_inc(end_step, 1)
                    n[0] += len(steps)
                    dve.wait_ge(end_step, n[0])

                combine(BLOCKS - 1, u)
                dve.wait_ge(both_done, BLOCKS)
                then(nc.vector.tensor_tensor(den[:, u, 0:1], both[:, u, D:DA], both[:, u, MV - 1:MV], ALU.add),
                     nc.vector.tensor_tensor(num[:, u, :], both[:, u, 0:D], both[:, u, DA:MV - 1], ALU.add))
                then(nc.vector.tensor_scalar(den[:, u, 1:2], den[:, u, 0:1], TINY, top_all[:, 4:5], ALU.max, ALU.mult),
                     nc.vector.tensor_scalar(den[:, u, 2:3], den[:, u, 0:1], 0.0, None, ALU.is_equal))
                dve.wait_ge(x_blk_in[u], PAIRS * 16)
                then(nc.vector.reciprocal(den[:, u, 3:4], den[:, u, 1:2]),
                     nc.vector.scalar_tensor_tensor(rest[:, u, :], h_mean[:], den[:, u, 2:3], x_blk[:, u, :], ALU.mult, ALU.add))
                dve.wait_ge(out_done[u], (PAIRS - 1) * 16)
                then(nc.vector.scalar_tensor_tensor(y_blk[:, u, :], num[:, u, :], den[:, u, 3:4], rest[:, u, :], ALU.mult, ALU.add))
                then(nc.vector.bn_stats(stats[:, u, :], y_blk[:, u, :]))
                nc.vector.bn_aggr(mv[:, u, 0:2], stats[:, u, :]).then_inc(y_done, 1)
                dve.wait_ge(std_done, 1)
                nc.vector.tensor_scalar(o_blk[:, u, :], y_blk[:, u, :], mv[:, u, 0:1], mv[:, u, 3:4],
                                        ALU.subtract, ALU.mult).then_inc(norm_done, 1)

_INS = ["x", "adj", "L0_gnn_W", "L0_gnn_b_W", "L0_gnn_a_vec", "L0_gnn_b_a"]


def kernel(**inputs):
    import numpy as _np
    import concourse.bacc as _bacc
    from concourse import mybir as _mybir
    from concourse.bass_utils import run_bass_kernel_spmd as _run

    nc = _bacc.Bacc("TRN2", target_bir_lowering=False, num_devices=1)
    arrays, args = {}, []
    for name in _INS:
        a = _np.ascontiguousarray(inputs[name])
        arrays[f"in_{name}"] = a
        args.append(nc.dram_tensor(f"in_{name}", a.shape, _mybir.dt.from_np(a.dtype), kind="ExternalInput").ap())
    n, d = inputs["x"].shape
    out = nc.dram_tensor("out_0", (n, d), _mybir.dt.float32, kind="ExternalOutput").ap()
    s_lin = nc.dram_tensor("s_lin", (2, n), _mybir.dt.float32, kind="Internal").ap()
    gat_kernel(nc, *args, out, s_lin)
    r = _run(nc, [arrays], core_ids=[0])
    return r.results[0]["out_0"]
```
